# Optimizing a Trainium2 kernel written in Bass

```python
import numpy as np
import jax
import jax.numpy as jnp

def _softmax(x, axis=-1):
    return jax.nn.softmax(x, axis=axis)

def _gelu(x):
    return jax.nn.gelu(x, approximate=True)

def _silu(x):
    return jax.nn.silu(x)

def _sigmoid(x):
    return jax.nn.sigmoid(x)

def _layernorm(x, axis=-1, eps=1e-05):
    m = jnp.mean(x, axis=axis, keepdims=True)
    v = jnp.var(x, axis=axis, keepdims=True)
    return (x - m) / jnp.sqrt(v + eps)

def _scatter_add(tgt, idx, src, axis=0):
    return tgt.at[idx].add(src)

def _segment_sum(src, seg, n):
    return jax.ops.segment_sum(src, seg, n)
kernel_name = 'mk_adaln_ffn_d1_seqx_r4_2dda2a'

def setup_inputs(seed: int=0):
    np.random.seed(seed)
    _w = jnp.asarray

    def _rec_inputs():
        import jax
        import jax.numpy as jnp
        _rk = jax.random.key(seed)
        x = -0.000125 + 0.9999 * jax.random.normal(jax.random.fold_in(_rk, 1), (32, 64, 1024), jnp.float32)
        _lenS = 64 - jax.random.randint(jax.random.fold_in(_rk, 7), (32,), 0, max(1, 64 // 4) + 1, jnp.int32)
        _lenS2 = 64 - jax.random.randint(jax.random.fold_in(_rk, 8), (32,), 0, max(1, 64 // 4) + 1, jnp.int32)
        itok_B_0_7 = jax.random.randint(jax.random.fold_in(_rk, 11), (32,), 0, 8, jnp.int32)
        return (x, itok_B_0_7)
    x, itok_B_0_7 = _rec_inputs()

    def _L0_cond_setup():
        import jax, jax.numpy as jnp
        import numpy as np
        TOP_K = 2
        LANG_BIAS = 5.0
        SCALING = 32.0 / 16.0
        LANGUAGE_PAD_ID = -1
        key = jax.random.key(seed)
        ks = jax.random.split(key, 6)
        B, T, D, O, E, R = (4, 512, 1024, 1024, 8, 16)
        x = jax.random.normal(ks[0], (B, T, D), dtype=jnp.float32)
        language_ids = jax.random.randint(ks[1], (B,), 0, E).astype(jnp.int64)
        W = jax.random.normal(ks[2], (O, D), dtype=jnp.float32) * (1.0 / np.sqrt(D))
        Wr = jax.random.normal(ks[3], (E, D), dtype=jnp.float32) * (1.0 / np.sqrt(D))
        A = jax.random.normal(ks[4], (E, R, D), dtype=jnp.float32) * (1.0 / np.sqrt(D))
        Bm = jax.random.normal(ks[5], (O, R), dtype=jnp.float32) * 0.0
        Bm = jnp.broadcast_to(Bm, (E, O, R)) + jax.random.normal(ks[5], (E, O, R), dtype=jnp.float32) * 0.02
        return {'x': x, 'language_ids': language_ids, 'W': W, 'Wr': Wr, 'A': A, 'B': Bm}
    _L0_cond_all = _L0_cond_setup()
    _L0_cond_in = {k: v for k, v in _L0_cond_all.items() if k in ('W', 'Wr', 'A', 'B')}
    del _L0_cond_all

    def _L0_ffn_setup():
        import jax, jax.numpy as jnp
        import numpy as np
        B_, S, D_IN, D_OUT = (4, 512, 1024, 1024)
        N, RANK, ALPHA = (8, 16, 32)
        SCALE = ALPHA / RANK
        key = jax.random.key(seed)
        kx, ka, kb, kw, kbias = jax.random.split(key, 5)
        x = jax.random.normal(kx, (B_, S, D_IN), dtype=jnp.float32)
        lora_A = jax.random.normal(ka, (N, RANK, D_IN), dtype=jnp.float32) * (1.0 / np.sqrt(D_IN))
        lora_B = jax.random.normal(kb, (N, D_OUT, RANK), dtype=jnp.float32) * (1.0 / np.sqrt(RANK))
        W = jax.random.normal(kw, (D_OUT, D_IN), dtype=jnp.float32) * (1.0 / np.sqrt(D_IN))
        bias = jax.random.normal(kbias, (D_OUT,), dtype=jnp.float32) * 0.01
        lora_weights = jnp.full((N,), 1.0 / N, dtype=jnp.float32)
        return {'x': x, 'lora_A': lora_A, 'lora_B': lora_B, 'W': W, 'bias': bias, 'lora_weights': lora_weights}
    _L0_ffn_all = _L0_ffn_setup()
    _L0_ffn_in = {k: v for k, v in _L0_ffn_all.items() if k in ('lora_A', 'lora_B', 'W', 'bias', 'lora_weights')}
    del _L0_ffn_all
    return {'x': x, 'itok_B_0_7': itok_B_0_7, 'L0_cond_W': _L0_cond_in['W'], 'L0_cond_Wr': _L0_cond_in['Wr'], 'L0_cond_A': _L0_cond_in['A'], 'L0_cond_B': _L0_cond_in['B'], 'L0_ffn_lora_A': _L0_ffn_in['lora_A'], 'L0_ffn_lora_B': _L0_ffn_in['lora_B'], 'L0_ffn_W': _L0_ffn_in['W'], 'L0_ffn_bias': _L0_ffn_in['bias'], 'L0_ffn_lora_weights': _L0_ffn_in['lora_weights']}

def reference(x, itok_B_0_7, L0_cond_W, L0_cond_Wr, L0_cond_A, L0_cond_B, L0_ffn_lora_A, L0_ffn_lora_B, L0_ffn_W, L0_ffn_bias, L0_ffn_lora_weights):
    import jax
    import jax.numpy as jnp

    def _L0_cond_ref(x, language_ids, W, Wr, A, B):
        import jax, jax.numpy as jnp
        import numpy as np
        TOP_K = 2
        LANG_BIAS = 5.0
        SCALING = 32.0 / 16.0
        LANGUAGE_PAD_ID = -1
        base = jnp.einsum('btd,od->bto', x, W)
        E = Wr.shape[0]
        logits = jnp.einsum('btd,ed->bte', x.astype(jnp.float32), Wr.astype(jnp.float32))
        expert_targets = language_ids
        valid = expert_targets >= 0
        tgt = jnp.where(valid, expert_targets, 0)
        bias = jax.nn.one_hot(tgt, E, dtype=logits.dtype) * LANG_BIAS
        bias = jnp.where(valid[:, None], bias, 0.0)
        logits = logits + bias[:, None, :]
        topw, topi = jax.lax.top_k(logits, TOP_K)
        weights = jax.nn.softmax(topw, axis=-1)
        gates = jnp.sum(jax.nn.one_hot(topi, E, dtype=weights.dtype) * weights[..., None], axis=-2)
        gates = gates.astype(x.dtype)
        h = jnp.einsum('btd,erd->bter', x, A)
        lora_out = jnp.einsum('bter,bte,eor->bto', h, gates, B)
        return base + SCALING * lora_out

    def _L0_ffn_ref(x, lora_A, lora_B, W, bias, lora_weights):
        import jax, jax.numpy as jnp
        import numpy as np
        B_, S, D_IN, D_OUT = (4, 512, 1024, 1024)
        N, RANK, ALPHA = (8, 16, 32)
        SCALE = ALPHA / RANK
        h = jnp.einsum('bsd,nrd->nbsr', x, lora_A)
        coef = (SCALE * lora_weights)[:, None, None]
        lora_out = jnp.einsum('nbsr,nor->bso', h, lora_B * coef)
        base = jnp.einsum('bsd,od->bso', x, W) + bias
        return base + lora_out
    x = x + _L0_ffn_ref(_L0_cond_ref(x, itok_B_0_7, L0_cond_W, L0_cond_Wr, L0_cond_A, L0_cond_B), L0_ffn_lora_A, L0_ffn_lora_B, L0_ffn_W, L0_ffn_bias, L0_ffn_lora_weights)
    return x

_drawn_inputs = setup_inputs


def setup_inputs(seed=0):
    import zlib

    import numpy as np

    out = dict(_drawn_inputs(seed))
    spreads = {'L0_ffn_lora_weights': (0.125, 0.2)}
    factors = {'L0_cond_Wr': 4.778, 'L0_ffn_bias': 8.0}
    for name, (base, spread) in spreads.items():
        noise = np.random.default_rng([zlib.crc32(name.encode()), seed]).standard_normal(out[name].shape)
        drawn = base * np.exp(spread * noise) if base else spread * noise
        out[name] = jnp.asarray(drawn.astype(out[name].dtype))
    for name, factor in factors.items():
        out[name] = (out[name] * factor).astype(out[name].dtype)
    return out
```

```python
import concourse.bass as bass
from concourse import mybir
from contextlib import ExitStack



ROWS, D = 2048, 1024
P = 128
KD = D // P
E, R = 8, 16
ER = E * R
HALF = 512
NH = D // HALF
TILE = 512
TILES = ROWS // TILE
SUBS = TILE // P
SEQ = 64
KM = KD + 1
GROUP = 3
GROUPS = KM // GROUP
HR = ER + E
LANG_BIAS = 5.0
SCALING = 2.0
BELOW = -3.0e38
RAW = 4
STAGES = 4
W_SLOT = [2, 3, 0]
X_SLOT = [1, 2, 3, 0]
M_BANKS = 6
C_BANK = [6, 7, 4, 5]
T_BANK = 6

FIRST = [("Af", 0, 1), ("Bf", 1, 1), ("F00", 2, 2), ("F01", 3, 2), ("W0", 0, 1), ("F02", 1, 2), ("W1", 2, 1),
         ("F03", 3, 2), ("W2", 0, 1), ("F10", 1, 2), ("F11", 2, 2), ("F12", 3, 2), ("F13", 0, 2), ("A", 1, 2)]


def adaln_ffn(nc, x, ids, w_blocks, wr, a, lora_a, lora_b, ffn_w, bias, lora_weights, out):
    f32, f32r, i32 = mybir.dt.float32, mybir.dt.float32r, mybir.dt.int32
    ALU = mybir.AluOpType
    ACT = mybir.ActivationFunctionType
    AX = mybir.AxisListType

    fill, split_from, split_to = {}, {}, {}
    fills, splits = [0] * RAW, 0
    for name, slot, n in FIRST:
        fills[slot] += 1
        fill[name], split_from[name] = 16 * fills[slot], splits
        splits += n
        split_to[name] = splits
    SPLITS_W = splits
    SPLITS_X = SPLITS_W + KM - GROUP
    FILLS_W = [fills[W_SLOT[j]] for j in range(GROUP)]
    FILLS_X = [fills[s] + (GROUPS - 1) * (s in W_SLOT) for s in X_SLOT]
    M_BLOCKS = KM * NH

    ctx = ExitStack()
    with ctx:
        def sb(name, shape, dt=f32):
            return ctx.enter_context(nc.sbuf_tensor(name, shape, dt))

        def sem(name):
            return ctx.enter_context(nc.semaphore(name))

        raw = sb("raw", [P, RAW, 1024])
        m_hi = sb("m_hi", [P, KM, D], f32r)
        m_lo = sb("m_lo", [P, KM, D], f32r)
        fx_hi = sb("fx_hi", [P, 2, KD, 512], f32r)
        fx_lo = sb("fx_lo", [P, 2, KD, 512], f32r)
        w_hi = sb("w_hi", [P, GROUP, KD, P], f32r)
        w_lo = sb("w_lo", [P, GROUP, KD, P], f32r)
        aw = sb("aw", [P, KD, 2 * HR], f32r)
        wr_raw = sb("wr_raw", [P, KD, E])
        g_hi = sb("g_hi", [P, TILE], f32r)
        g_lo = sb("g_lo", [P, TILE], f32r)
        stage = sb("stage", [P, STAGES, TILE])
        h_part = sb("h_part", [P, SUBS, HR])
        hl = sb("hl", [P, SUBS, HR])
        gh = sb("gh", [P, SUBS, ER])
        ident = sb("ident", [P, P])
        coef = sb("coef", [P, 1])
        bias_col = sb("bias_col", [P, KD])
        ids_raw = sb("ids_raw", [P, ROWS // P], i32)
        ids_rank = sb("ids_rank", [P, ROWS // P])
        rank = sb("rank", [P, ROWS // P, E])
        lang = sb("lang", [P, ROWS // P, E])
        logits = sb("logits", [P, SUBS, E])
        rest = sb("rest", [P, SUBS, E])
        hit = sb("hit", [P, 2, SUBS, E])
        score = sb("score", [P, 2, SUBS, E])
        best = sb("best", [P, 2, SUBS])
        top = sb("top", [P, 2, SUBS])
        first = sb("first", [P, SUBS, E])
        second = sb("second", [P, SUBS, E])
        gap = sb("gap", [P, SUBS])
        expo = sb("expo", [P, SUBS])
        denom = sb("denom", [P, SUBS])
        inv = sb("inv", [P, SUBS])
        weight = sb("weight", [P, 2, SUBS])
        part = sb("part", [P, 2, SUBS, E])
        gates = sb("gates", [P, SUBS, E])

        ps = ctx.enter_context(nc.psum_tensor("ps", [P, 8, 512], f32))

        af_hi, af_lo = m_hi[:, KM - 1, :], m_lo[:, KM - 1, :]
        bf_hi, bf_lo = m_hi[:, KM - 2, :], m_lo[:, KM - 2, :]

        raw_loaded = [sem(f"raw_loaded{s}") for s in range(RAW)]
        coef_loaded = sem("coef_loaded")
        wr_loaded = sem("wr_loaded")
        ids_loaded = sem("ids_loaded")
        bias_loaded = sem("bias_loaded")
        bf_scaled = sem("bf_scaled")
        hi_done = sem("hi_done")
        lo_done = sem("lo_done")
        ft_product = sem("ft_product")
        ft_added = sem("ft_added")
        m_product = sem("m_product")
        m_hi_done = sem("m_hi_done")
        bank_read = sem("bank_read")
        ident_zero = sem("ident_zero")
        ident_ready = sem("ident_ready")
        rank_ready = sem("rank_ready")
        ids_ready = sem("ids_ready")
        lang_hit = sem("lang_hit")
        lang_ready = sem("lang_ready")
        h_product = sem("h_product")
        h_part_read = sem("h_part_read")
        hl_ready = sem("hl_ready")
        logits_ready = sem("logits_ready")
        top_ready = [sem(f"top_ready{i}") for i in range(2)]
        hit_ready = [sem(f"hit_ready{i}") for i in range(2)]
        score_ready = [sem(f"score_ready{i}") for i in range(2)]
        best_ready = [sem(f"best_ready{i}") for i in range(2)]
        chosen = [sem(f"chosen{i}") for i in range(2)]
        rest_ready = sem("rest_ready")
        gap_ready = sem("gap_ready")
        expo_ready = sem("expo_ready")
        denom_ready = sem("denom_ready")
        inv_ready = sem("inv_ready")
        weight_ready = [sem(f"weight_ready{i}") for i in range(2)]
        part_ready = sem("part_ready")
        gates_ready = sem("gates_ready")
        gh_ready = sem("gh_ready")
        g_turned = sem("g_turned")
        g_hi_done = sem("g_hi_done")
        g_lo_done = sem("g_lo_done")
        out_product = sem("out_product")
        x_staged = sem("x_staged")
        stage_free = [sem(f"stage_free{s}") for s in range(STAGES)]

        block = ctx.enter_context(nc.Block())

        @block.sync
        def _(sp):
            dram = {"Af": lora_a, "Bf": lora_b, "A": a}
            for d in range(GROUP):
                dram[f"W{d}"] = w_blocks[d]
            for h in range(NH):
                for q in range(KD // 2):
                    dram[f"F{h}{q}"] = ffn_w[h, q]
            last_in = {}
            for name, slot, _ in FIRST:
                if slot in last_in:
                    sp.wait_ge(lo_done, split_to[last_in[slot]])
                sp.dma_start(raw[:, slot, :], dram[name]).then_inc(raw_loaded[slot], 16)
                last_in[slot] = name
                if name == "Bf":
                    sp.dma_start(coef[:, :], lora_weights.rearrange("(e a) -> e a", a=1)
                                 .unsqueeze(1).to_broadcast([E, R, 1])).then_inc(coef_loaded, 16)
                if name == "F13":
                    sp.dma_start(wr_raw[:, :, :], wr).then_inc(wr_loaded, 16)
                    for b in range(P // SEQ):
                        sp.dma_start(ids_raw[SEQ * b:SEQ * (b + 1), :], ids[b, :].partition_broadcast(SEQ))\
                          .then_inc(ids_loaded, 16)
                    sp.dma_start(bias_col[:, :], bias).then_inc(bias_loaded, 16)
            with sp.Fori(1, GROUPS) as g:
                for j in range(GROUP):
                    sp.wait_ge(lo_done, SPLITS_W + GROUP * (g - 2) + j + 1)
                    sp.dma_start(raw[:, W_SLOT[j], :], w_blocks[bass.ds(GROUP * g + j, 1), :, :]
                                 .rearrange("a p n -> (a p) n")).then_inc(raw_loaded[W_SLOT[j]], 16)

            def load_x(t):
                for i in range(4):
                    sp.wait_ge(lo_done, SPLITS_X + 4 * t + i - 3)
                    sp.dma_start(raw[:, X_SLOT[i], :], x[bass.ds(4 * t + i, 1), :, :]
                                 .rearrange("a p n -> (a p) n")).then_inc(raw_loaded[X_SLOT[i]], 16)

            def store(t):
                for ob in range(KD):
                    sp.wait_ge(bank_read, M_BLOCKS + KD * t + ob + 1)
                    sp.dma_start(out[bass.ds(KD * t + ob, 1), :, :].rearrange("a p n -> (a p) n"),
                                 stage[:, ob % STAGES, :]).then_inc(stage_free[ob % STAGES], 16)

            load_x(0)
            with sp.Fori(0, TILES - 1) as t:
                load_x(t + 1)
                store(t)
            store(TILES - 1)
            for s in range(STAGES):
                sp.wait_ge(stage_free[s], 16 + 16 * TILES * KD // STAGES)

        @block.scalar
        def _(act):
            def hi_first(name, dst):
                slot = next(s for n, s, _ in FIRST if n == name)
                act.wait_ge(raw_loaded[slot], fill[name])
                nc.scalar.activation(dst, raw[:, slot, :], ACT.Copy).then_inc(hi_done, 1)

            def hi_ft(h, q):
                slot = next(s for n, s, _ in FIRST if n == f"F{h}{q}")
                for i in range(2):
                    c = 2 * q + i
                    act.wait_ge(ft_added, KD * h + c + 1)
                    nc.scalar.activation(fx_hi[:, h, c, :], raw[:, slot, i * HALF:(i + 1) * HALF],
                                         ACT.Copy).then_inc(hi_done, 1)

            def hi_m(n, d, h, b):
                act.wait_ge(m_product, n + 1)
                nc.scalar.activation(m_hi[:, bass.ds(d, 1), h * HALF:(h + 1) * HALF].rearrange("p a n -> p (a n)"),
                                     ps[:, b, :], ACT.Copy).then_inc(m_hi_done, 1)

            def hi_w(g, j):
                act.wait_ge(raw_loaded[W_SLOT[j]], 16 * FILLS_W[j] + 16 * g)
                nc.scalar.activation(w_hi[:, j, :, :].rearrange("p c n -> p (c n)"), raw[:, W_SLOT[j], :],
                                     ACT.Copy).then_inc(hi_done, 1)

            def hi_x(t, i, parity):
                act.wait_ge(raw_loaded[X_SLOT[i]], 16 * FILLS_X[i] + 16 * (t + 1))
                dst = fx_hi[:, bass.ds(parity, 1), 2 * i:2 * i + 2, :].rearrange("p a c n -> p (a c n)")
                nc.scalar.activation(dst, raw[:, X_SLOT[i], :], ACT.Copy).then_inc(hi_done, 1)

            hi_first("Af", af_hi)
            act.wait_ge(bf_scaled, 1)
            hi_first("Bf", bf_hi)
            hi_ft(0, 0)
            hi_ft(0, 1)
            hi_first("W0", w_hi[:, 0, :, :].rearrange("p c n -> p (c n)"))
            hi_ft(0, 2)
            hi_first("W1", w_hi[:, 1, :, :].rearrange("p c n -> p (c n)"))
            hi_ft(0, 3)
            hi_first("W2", w_hi[:, 2, :, :].rearrange("p c n -> p (c n)"))
            hi_m(0, 0, 0, 0)
            hi_ft(1, 0)
            hi_ft(1, 1)
            hi_m(1, 1, 0, 1)
            hi_ft(1, 2)
            hi_ft(1, 3)
            hi_m(2, 2, 0, 2)
            act.wait_ge(raw_loaded[1], fill["A"])
            nc.scalar.activation(aw[:, :, 0:ER], raw[:, 1, :].rearrange("p (c n) -> p c n", c=KD),
                                 ACT.Copy).then_inc(hi_done, 1)
            act.wait_ge(wr_loaded, 16)
            nc.scalar.activation(aw[:, :, ER:HR], wr_raw[:, :, :], ACT.Copy).then_inc(hi_done, 1)
            with act.Fori(1, GROUPS) as g:
                for j in range(GROUP):
                    hi_m(2 * GROUP * g - GROUP + j, GROUP * (g - 1) + j, 1, GROUP + j)
                    hi_w(g, j)
                for j in range(GROUP):
                    hi_m(2 * GROUP * g + j, GROUP * g + j, 0, j)
            for j in range(GROUP):
                for i in ((0, 1), (2,), (3,))[j]:
                    hi_x(0, i, 0)
                hi_m(M_BLOCKS - GROUP + j, KM - GROUP + j, 1, GROUP + j)

            def window(t):
                for s in range(SUBS):
                    act.wait_ge(h_product, SUBS * t + s + 1)
                    nc.scalar.activation(h_part[:, s, :], ps[:, C_BANK[s], HR:2 * HR], ACT.Copy)\
                      .then_inc(h_part_read, 1)
                act.wait_ge(gap_ready, t + 1)
                nc.scalar.activation(expo[:, :], gap[:, :], ACT.Exp).then_inc(expo_ready, 1)
                act.wait_ge(g_turned, t + 1)
                nc.scalar.activation(g_hi[:, :], ps[:, T_BANK, :], ACT.Copy).then_inc(g_hi_done, 1)

            with act.Fori(0, TILES - 1) as t:
                window(t)
                for i in range(4):
                    hi_x(t + 1, i, (t + 1) % 2)
            window(TILES - 1)

        @block.gpsimd
        def _(pool):
            sub = ALU.subtract

            def lo(n, dst, src, hi):
                pool.wait_ge(hi_done, n)
                nc.gpsimd.tensor_tensor(dst, src, hi.bitcast(f32), sub).then_inc(lo_done, 1)

            for s in range(STAGES):
                pool.sem_inc(stage_free[s], 16)
            nc.gpsimd.memset(ident[:, :], 0.0).then_inc(ident_zero, 1)
            pool.wait_ge(ident_zero, 1)
            nc.gpsimd.affine_select(out=ident[:, :], in_=ident[:, :], compare_op=ALU.not_equal, fill=1.0,
                                    base=0, pattern=[[-1, P]], channel_multiplier=1).then_inc(ident_ready, 1)
            n = 0
            for name, slot, _ in FIRST:
                if name[0] == "F":
                    h, q = int(name[1]), int(name[2])
                    for i in range(2):
                        n += 1
                        lo(n, fx_lo[:, h, 2 * q + i, :], raw[:, slot, i * HALF:(i + 1) * HALF],
                           fx_hi[:, h, 2 * q + i, :])
                elif name[0] == "W":
                    n += 1
                    j = int(name[1])
                    lo(n, w_lo[:, j, :, :].rearrange("p c n -> p (c n)"), raw[:, slot, :],
                       w_hi[:, j, :, :].rearrange("p c n -> p (c n)"))
                elif name == "A":
                    lo(n + 1, aw[:, :, HR:HR + ER], raw[:, slot, :].rearrange("p (c n) -> p c n", c=KD),
                       aw[:, :, 0:ER])
                    lo(n + 2, aw[:, :, HR + ER:2 * HR], wr_raw[:, :, :], aw[:, :, ER:HR])
                    n += 2
                else:
                    n += 1
                    lo(n, af_lo if name == "Af" else bf_lo, raw[:, slot, :], af_hi if name == "Af" else bf_hi)
            with pool.Fori(1, GROUPS) as g:
                for j in range(GROUP):
                    lo(SPLITS_W + GROUP * (g - 1) + j + 1, w_lo[:, j, :, :].rearrange("p c n -> p (c n)"),
                       raw[:, W_SLOT[j], :], w_hi[:, j, :, :].rearrange("p c n -> p (c n)"))

            with pool.Fori(0, TILES // 2) as pair:
                for par in range(2):
                    t = 2 * pair + par
                    for i in range(4):
                        lo(SPLITS_X + 4 * t + i + 1, fx_lo[:, par, 2 * i:2 * i + 2, :].rearrange("p c n -> p (c n)"),
                           raw[:, X_SLOT[i], :], fx_hi[:, par, 2 * i:2 * i + 2, :].rearrange("p c n -> p (c n)"))
                    pool.wait_ge(lo_done, SPLITS_X + 4 * t + 4)
                    for ob in range(KD):
                        pool.wait_ge(stage_free[ob % STAGES], 16 * (KD // STAGES) * t + 16 * (ob // STAGES + 1))
                        nc.gpsimd.tensor_tensor(stage[:, ob % STAGES, :], fx_hi[:, par, ob, :].bitcast(f32),
                                                fx_lo[:, par, ob, :].bitcast(f32), ALU.add).then_inc(x_staged, 1)

        @block.vector
        def _(dve):
            mult, add, eq = ALU.mult, ALU.add, ALU.is_equal
            dve.wait_ge(raw_loaded[1], fill["Bf"])
            dve.wait_ge(coef_loaded, 16)
            nc.vector.tensor_scalar(raw[:, 1, :], raw[:, 1, :], coef[:, 0:1], SCALING, mult, mult)\
              .then_inc(bf_scaled, 1)

            def add_ft(h, q):
                slot = next(s for n, s, _ in FIRST if n == f"F{h}{q}")
                dve.wait_ge(raw_loaded[slot], fill[f"F{h}{q}"])
                for c in (2 * q, 2 * q + 1):
                    half = raw[:, slot, (c % 2) * HALF:(c % 2 + 1) * HALF]
                    dve.wait_ge(ft_product, KD * h + c + 1)
                    nc.vector.tensor_tensor(half, ps[:, 4 + c % 4, :], half, add).then_inc(ft_added, 1)

            def lo_m(n, d, h, b):
                cols = m_hi[:, bass.ds(d, 1), h * HALF:(h + 1) * HALF].rearrange("p a n -> p (a n)")
                dst = m_lo[:, bass.ds(d, 1), h * HALF:(h + 1) * HALF].rearrange("p a n -> p (a n)")
                dve.wait_ge(m_hi_done, n + 1)
                nc.vector.tensor_tensor(dst, ps[:, b, :], cols.bitcast(f32), ALU.subtract).then_inc(bank_read, 1)

            for q in range(4):
                add_ft(0, q)
            lo_m(0, 0, 0, 0)
            add_ft(1, 0)
            add_ft(1, 1)
            lo_m(1, 1, 0, 1)
            add_ft(1, 2)
            add_ft(1, 3)
            lo_m(2, 2, 0, 2)
            for e in range(E):
                ins = nc.vector.memset(rank[:, :, e:e + 1], float(E - e))
            ins.then_inc(rank_ready, 1)
            dve.wait_ge(ids_loaded, 16 * P // SEQ)
            nc.vector.tensor_scalar(ids_rank[:, :], ids_raw[:, :], -1.0, float(E), mult, add).then_inc(ids_ready, 1)
            dve.wait_ge(rank_ready, 1)
            dve.wait_ge(ids_ready, 1)
            nc.vector.tensor_tensor(lang[:, :, :], rank[:, :, :],
                                    ids_rank[:, :].unsqueeze(2).to_broadcast([P, ROWS // P, E]), eq)\
              .then_inc(lang_hit, 1)
            dve.wait_ge(lang_hit, 1)
            nc.vector.tensor_scalar(lang[:, :, :], lang[:, :, :], LANG_BIAS, None, mult).then_inc(lang_ready, 1)
            with dve.Fori(1, GROUPS) as g:
                for j in range(GROUP):
                    lo_m(2 * GROUP * g - GROUP + j, GROUP * (g - 1) + j, 1, GROUP + j)
                for j in range(GROUP):
                    lo_m(2 * GROUP * g + j, GROUP * g + j, 0, j)
            for j in range(GROUP):
                lo_m(M_BLOCKS - GROUP + j, KM - GROUP + j, 1, GROUP + j)
            dve.wait_ge(lang_ready, 1)
            dve.wait_ge(bias_loaded, 16)

            def spread(v):
                return v.unsqueeze(2).to_broadcast([P, SUBS, E])

            def choose(t, i, src):
                nc.vector.tensor_reduce(top[:, i, :], src[:, :, :], AX.X, ALU.max).then_inc(top_ready[i], 1)
                dve.wait_ge(top_ready[i], t + 1)
                nc.vector.tensor_tensor(hit[:, i, :, :], src[:, :, :], spread(top[:, i, :]), eq)\
                  .then_inc(hit_ready[i], 1)
                dve.wait_ge(hit_ready[i], t + 1)
                nc.vector.tensor_tensor(score[:, i, :, :], hit[:, i, :, :], rank[:, 0:SUBS, :], mult)\
                  .then_inc(score_ready[i], 1)
                dve.wait_ge(score_ready[i], t + 1)
                nc.vector.tensor_reduce(best[:, i, :], score[:, i, :, :], AX.X, ALU.max).then_inc(best_ready[i], 1)
                dve.wait_ge(best_ready[i], t + 1)
                nc.vector.tensor_tensor((first, second)[i][:, :, :], score[:, i, :, :], spread(best[:, i, :]), eq)\
                  .then_inc(chosen[i], 1)
                dve.wait_ge(chosen[i], t + 1)

            def window(t):
                for s in range(SUBS):
                    dve.wait_ge(h_part_read, SUBS * t + s + 1)
                    nc.vector.tensor_tensor(hl[:, s, :], ps[:, C_BANK[s], 0:HR], h_part[:, s, :], add)\
                      .then_inc(hl_ready, 1)
                dve.wait_ge(hl_ready, SUBS * t + SUBS)
                nc.vector.tensor_tensor(logits[:, :, :], hl[:, :, ER:HR], lang[:, bass.ds(SUBS * t, SUBS), :], add)\
                  .then_inc(logits_ready, 1)
                dve.wait_ge(logits_ready, t + 1)
                choose(t, 0, logits)
                nc.vector.scalar_tensor_tensor(out=rest[:, :, :], in0=first[:, :, :], scalar=BELOW,
                                               in1=logits[:, :, :], op0=mult, op1=add).then_inc(rest_ready, 1)
                dve.wait_ge(rest_ready, t + 1)
                choose(t, 1, rest)
                nc.vector.tensor_tensor(gap[:, :], top[:, 1, :], top[:, 0, :], ALU.subtract).then_inc(gap_ready, 1)
                dve.wait_ge(expo_ready, t + 1)
                nc.vector.tensor_scalar(denom[:, :], expo[:, :], 1.0, None, add).then_inc(denom_ready, 1)
                dve.wait_ge(denom_ready, t + 1)
                nc.vector.reciprocal(inv[:, :], denom[:, :]).then_inc(inv_ready, 1)
                dve.wait_ge(inv_ready, t + 1)
                nc.vector.tensor_scalar(weight[:, 0, :], inv[:, :], SCALING, None, mult).then_inc(weight_ready[0], 1)
                dve.wait_ge(weight_ready[0], t + 1)
                nc.vector.tensor_tensor(weight[:, 1, :], expo[:, :], weight[:, 0, :], mult)\
                  .then_inc(weight_ready[1], 1)
                dve.wait_ge(weight_ready[1], t + 1)
                for i in range(2):
                    ins = nc.vector.tensor_tensor(part[:, i, :, :], (first, second)[i][:, :, :],
                                                  spread(weight[:, i, :]), mult)
                ins.then_inc(part_ready, 1)
                dve.wait_ge(part_ready, t + 1)
                nc.vector.tensor_tensor(gates[:, :, :], part[:, 0, :, :], part[:, 1, :, :], add)\
                  .then_inc(gates_ready, 1)
                dve.wait_ge(gates_ready, t + 1)
                for s in range(SUBS):
                    ins = nc.vector.tensor_tensor(
                        gh[:, s, :].rearrange("p (e r) -> p e r", r=R),
                        hl[:, s, 0:ER].rearrange("p (e r) -> p e r", r=R),
                        gates[:, s, :].unsqueeze(2).to_broadcast([P, E, R]), mult)
                ins.then_inc(gh_ready, 1)
                dve.wait_ge(g_hi_done, t + 1)
                nc.vector.tensor_tensor(g_lo[:, :], ps[:, T_BANK, :], g_hi[:, :].bitcast(f32), ALU.subtract)\
                  .then_inc(g_lo_done, 1)
                for ob in range(KD):
                    dve.wait_ge(out_product, KD * t + ob + 1)
                    dve.wait_ge(x_staged, KD * t + ob + 1)
                    st = stage[:, ob % STAGES, :]
                    nc.vector.scalar_tensor_tensor(out=st, in0=ps[:, ob % 4, :], scalar=bias_col[:, ob:ob + 1],
                                                   in1=st, op0=add, op1=add).then_inc(bank_read, 1)

            with dve.Fori(0, TILES) as t:
                window(t)

        @block.tensor
        def _(pe):
            def ft(h, c):
                n = KD * h + c
                if n >= 4:
                    pe.wait_ge(ft_added, n - 3)
                cols, half = slice(c * P, (c + 1) * P), slice(h * HALF, (h + 1) * HALF)
                dst = ps[:, 4 + c % 4, :]
                nc.tensor.matmul(dst, af_lo[:, cols], bf_hi[:, half], start=True, stop=False)
                nc.tensor.matmul(dst, af_hi[:, cols], bf_lo[:, half], start=False, stop=False)
                nc.tensor.matmul(dst, af_hi[:, cols], bf_hi[:, half], start=False, stop=True).then_inc(ft_product, 1)

            def m_block(j, h, b, arriving=False):
                for c in range(KD):
                    if arriving:
                        pe.wait_ge(lo_done, split_from[f"F{h}{c // 2}"] + c % 2 + 1)
                    nc.tensor.matmul(ps[:, b, :], w_lo[:, j, c, :], fx_hi[:, h, c, :], start=(c == 0), stop=False)
                    nc.tensor.matmul(ps[:, b, :], w_hi[:, j, c, :], fx_lo[:, h, c, :], start=False, stop=False)
                for c in range(KD):
                    ins = nc.tensor.matmul(ps[:, b, :], w_hi[:, j, c, :], fx_hi[:, h, c, :],
                                           start=False, stop=(c == KD - 1))
                ins.then_inc(m_product, 1)

            pe.wait_ge(lo_done, split_to["Bf"])
            for c in range(KD):
                ft(0, c)
            pe.wait_ge(lo_done, split_to["W0"])
            m_block(0, 0, 0, arriving=True)
            for c in range(4):
                ft(1, c)
            pe.wait_ge(lo_done, split_to["W1"])
            m_block(1, 0, 1)
            for c in range(4, KD):
                ft(1, c)
            pe.wait_ge(lo_done, split_to["W2"])
            m_block(2, 0, 2)
            pe.wait_ge(ft_added, NH * KD)
            for j in range(GROUP):
                m_block(j, 1, GROUP + j, arriving=(j == 0))
            with pe.Fori(1, GROUPS) as g:
                for h in range(NH):
                    for j in range(GROUP):
                        if h == 0:
                            pe.wait_ge(lo_done, SPLITS_W + GROUP * (g - 1) + j + 1)
                        pe.wait_ge(bank_read, 2 * GROUP * (g - 1) + GROUP * h + j + 1)
                        m_block(j, h, GROUP * h + j)

            def h_and_logits(t, par):
                for s in range(SUBS):
                    rows, dst = slice(s * P, (s + 1) * P), ps[:, C_BANK[s], 0:2 * HR]
                    if s == 2:
                        pe.wait_ge(bank_read, M_BLOCKS)
                    for c in range(KD):
                        if s == 0 and c % 2 == 0:
                            pe.wait_ge(lo_done, SPLITS_X + 4 * t + c // 2 + 1)
                        nc.tensor.matmul(dst, fx_hi[:, par, c, rows], aw[:, c, :], start=(c == 0), stop=False)
                        ins = nc.tensor.matmul(dst[:, HR:2 * HR], fx_lo[:, par, c, rows], aw[:, c, 0:HR],
                                               start=False, stop=(c == KD - 1))
                    ins.then_inc(h_product, 1)

            def features(t, ob, par):
                cols, dst = slice(ob * P, (ob + 1) * P), ps[:, ob % 4, :]
                pe.wait_ge(bank_read, M_BLOCKS - 3 + KD * t + ob)
                for c in range(KD):
                    nc.tensor.matmul(dst, m_lo[:, c, cols], fx_hi[:, par, c, :], start=(c == 0), stop=False)
                    nc.tensor.matmul(dst, m_hi[:, c, cols], fx_lo[:, par, c, :], start=False, stop=False)
                for c in range(KD):
                    nc.tensor.matmul(dst, m_hi[:, c, cols], fx_hi[:, par, c, :], start=False, stop=False)

            def turn(t):
                pe.wait_ge(gh_ready, t + 1)
                for s in range(SUBS):
                    ins = nc.tensor.transpose(ps[:, T_BANK, s * P:(s + 1) * P], gh[:, s, :], ident[:, :])
                ins.then_inc(g_turned, 1)

            def ranks(ob):
                cols, dst = slice(ob * P, (ob + 1) * P), ps[:, ob % 4, :]
                nc.tensor.matmul(dst, m_lo[:, KD, cols], g_hi[:, :], start=False, stop=False)
                nc.tensor.matmul(dst, m_hi[:, KD, cols], g_lo[:, :], start=False, stop=False)
                nc.tensor.matmul(dst, m_hi[:, KD, cols], g_hi[:, :], start=False, stop=True)\
                  .then_inc(out_product, 1)

            pe.wait_ge(ident_ready, 1)
            with pe.Fori(0, TILES // 2) as pair:
                for par in range(2):
                    t = 2 * pair + par
                    h_and_logits(t, par)
                    for ob in range(KD):
                        features(t, ob, par)
                        if ob == 1:
                            turn(t)
                        if ob == 2:
                            pe.wait_ge(g_lo_done, t + 1)
                        if ob >= 2:
                            ranks(ob - 2)
                    ranks(KD - 2)
                    ranks(KD - 1)


def kernel(x, itok_B_0_7, L0_cond_W, L0_cond_Wr, L0_cond_A, L0_cond_B, L0_ffn_lora_A, L0_ffn_lora_B, L0_ffn_W,
           L0_ffn_bias, L0_ffn_lora_weights):
    import numpy as np
    import concourse.bacc as bacc
    from concourse.bass_utils import run_bass_kernel_spmd

    n = np.asarray
    xt = n(x).reshape(TILES, TILE, KD // 2, 2, P).transpose(0, 2, 4, 3, 1).reshape(-1, P, 1024)
    w = n(L0_cond_W).reshape(KD, P, KD, P).transpose(2, 1, 0, 3).reshape(KD, P, 1024)
    b = n(L0_cond_B).transpose(1, 0, 2).reshape(KD, P, ER).transpose(1, 0, 2).reshape(1, P, 1024)
    arrays = {
        "x": xt,
        "ids": n(itok_B_0_7).reshape(-1, P // SEQ).T,
        "w_blocks": np.concatenate([w, b]),
        "wr": n(L0_cond_Wr).reshape(E, KD, P).transpose(2, 1, 0),
        "a": n(L0_cond_A).reshape(ER, KD, P).transpose(2, 1, 0).reshape(P, 1024),
        "lora_a": n(L0_ffn_lora_A).reshape(ER, D),
        "lora_b": n(L0_ffn_lora_B).transpose(0, 2, 1).reshape(ER, D),
        "ffn_w": n(L0_ffn_W).reshape(NH, HALF, KD // 2, 2, P).transpose(0, 2, 4, 3, 1).reshape(NH, KD // 2, P, 1024),
        "bias": n(L0_ffn_bias).reshape(KD, P).T,
        "lora_weights": n(L0_ffn_lora_weights),
    }
    nc = bacc.Bacc("TRN2", target_bir_lowering=False, num_devices=1)
    args, given = [], {}
    for name, v in arrays.items():
        v = np.ascontiguousarray(v)
        given[f"in_{name}"] = v
        args.append(nc.dram_tensor(f"in_{name}", v.shape, mybir.dt.from_np(v.dtype), kind="ExternalInput").ap())
    args.append(nc.dram_tensor("out_t", (TILES * KD, P, TILE), mybir.dt.float32, kind="ExternalOutput").ap())
    adaln_ffn(nc, *args)
    got = run_bass_kernel_spmd(nc, [given], core_ids=[0]).results[0]["out_t"]
    return got.reshape(TILES, KD, P, TILE).transpose(0, 3, 1, 2).reshape(n(x).shape)
```

```python
import concourse.bass as bass
from concourse import mybir
from contextlib import ExitStack



ROWS, D = 2048, 1024
P = 128
KD = D // P
E, R = 8, 16
ER = E * R
HALF = 512
NH = D // HALF
TILE = 512
TILES = ROWS // TILE
SUBS = TILE // P
SEQ = 64
KM = KD + 1
GROUP = 3
GROUPS = KM // GROUP
HR = ER + E
LANG_BIAS = 5.0
SCALING = 2.0
BELOW = -3.0e38
RAW = 4
STAGES = 4
M_BANKS = 6
C_BANK = [6, 7, 4, 5]
T_BANK = 6
FT_BANK = [4, 5, 6, 7, 1, 2, 3, 4] + [4 + (n - 7) % 4 for n in range(8, 16)]
WARM_UP = 8

PIECES = [("F00", 0), ("W0", 1), ("F01", 2), ("F02", 3), ("F03", 0), ("W1", 1), ("W2", 2),
          ("F10", 3), ("F11", 0), ("F12", 1), ("F13", 2), ("A", 3)]
X_SLOT = [3, 0, 1, 2]


def adaln_ffn(nc, x, ids, w_blocks, wr, a, lora_a, lora_b, ffn_w, bias, lora_weights, out):
    f32, f32r, i32 = mybir.dt.float32, mybir.dt.float32r, mybir.dt.int32
    ALU = mybir.AluOpType
    ACT = mybir.ActivationFunctionType
    AX = mybir.AxisListType

    slot_of, loaded = {}, {}
    fills = [0] * RAW
    for name, slot in PIECES:
        fills[slot] += 1
        slot_of[name], loaded[name] = slot, 16 * fills[slot]
    FILLS_X = [fills[s] + (GROUPS - 1) * (s < GROUP) for s in X_SLOT]
    M_BLOCKS = KM * NH

    ctx = ExitStack()
    with ctx:
        def sb(name, shape, dt=f32):
            return ctx.enter_context(nc.sbuf_tensor(name, shape, dt))

        def sem(name):
            return ctx.enter_context(nc.semaphore(name))

        raw = sb("raw", [P, RAW, 1024])
        m_hi = sb("m_hi", [P, KM, D], f32r)
        m_lo = sb("m_lo", [P, KM, D], f32r)
        fx_hi = sb("fx_hi", [P, 2, KD, 512], f32r)
        fx_lo = sb("fx_lo", [P, 2, KD, 512], f32r)
        w_hi = sb("w_hi", [P, GROUP, KD, P], f32r)
        w_lo = sb("w_lo", [P, GROUP, KD, P], f32r)
        aw = sb("aw", [P, KD, 2 * HR], f32r)
        wr_raw = sb("wr_raw", [P, KD, E])
        g_hi = sb("g_hi", [P, TILE], f32r)
        g_lo = sb("g_lo", [P, TILE], f32r)
        stage = sb("stage", [P, STAGES, TILE])
        h_part = sb("h_part", [P, SUBS, HR])
        hl = sb("hl", [P, SUBS, HR])
        gh = sb("gh", [P, SUBS, ER])
        ident = sb("ident", [P, P])
        coef = sb("coef", [P, 1])
        bias_col = sb("bias_col", [P, KD])
        ids_raw = sb("ids_raw", [P, ROWS // P], i32)
        ids_rank = sb("ids_rank", [P, ROWS // P])
        rank = sb("rank", [P, ROWS // P, E])
        lang = sb("lang", [P, ROWS // P, E])
        logits = sb("logits", [P, SUBS, E])
        rest = sb("rest", [P, SUBS, E])
        hit = sb("hit", [P, 2, SUBS, E])
        score = sb("score", [P, 2, SUBS, E])
        best = sb("best", [P, 2, SUBS])
        top = sb("top", [P, 2, SUBS])
        first = sb("first", [P, SUBS, E])
        second = sb("second", [P, SUBS, E])
        gap = sb("gap", [P, SUBS])
        expo = sb("expo", [P, SUBS])
        denom = sb("denom", [P, SUBS])
        inv = sb("inv", [P, SUBS])
        weight = sb("weight", [P, 2, SUBS])
        part = sb("part", [P, 2, SUBS, E])
        gates = sb("gates", [P, SUBS, E])

        ps = ctx.enter_context(nc.psum_tensor("ps", [P, 8, 512], f32))

        af_hi, af_lo = m_hi[:, KM - 1, :], m_lo[:, KM - 1, :]
        bf_hi, bf_lo = m_hi[:, KM - 2, :], m_lo[:, KM - 2, :]
        AF_STAGE, BF_STAGE = [0, 2], [1, 3]
        halves = [slice(h * HALF, (h + 1) * HALF) for h in range(NH)]

        raw_loaded = [sem(f"raw_loaded{s}") for s in range(RAW)]
        af_loaded = [sem(f"af_loaded{h}") for h in range(NH)]
        bf_loaded = [sem(f"bf_loaded{h}") for h in range(NH)]
        coef_loaded = sem("coef_loaded")
        wr_loaded = sem("wr_loaded")
        ids_loaded = sem("ids_loaded")
        bias_loaded = sem("bias_loaded")
        af_hi_done, af_lo_done = sem("af_hi_done"), sem("af_lo_done")
        bf_hi_done, bf_lo_done = sem("bf_hi_done"), sem("bf_lo_done")
        ft_hi_done = sem("ft_hi_done")
        ft0_even_lo = sem("ft0_even_lo")
        ft0_odd_lo = sem("ft0_odd_lo")
        ft1_lo = sem("ft1_lo")
        w_hi_done, w_lo_done = sem("w_hi_done"), sem("w_lo_done")
        w0_front_lo = sem("w0_front_lo")
        aw_hi_done, aw_lo_done = sem("aw_hi_done"), sem("aw_lo_done")
        x_hi_done, x_lo_done = sem("x_hi_done"), sem("x_lo_done")
        ft_product = sem("ft_product")
        ft_added = sem("ft_added")
        m_product = sem("m_product")
        m_hi_done = sem("m_hi_done")
        bank_read = sem("bank_read")
        ident_zero = sem("ident_zero")
        ident_ready = sem("ident_ready")
        rank_ready = sem("rank_ready")
        ids_ready = sem("ids_ready")
        lang_hit = sem("lang_hit")
        lang_ready = sem("lang_ready")
        h_product = sem("h_product")
        h_part_read = sem("h_part_read")
        hl_ready = sem("hl_ready")
        logits_ready = sem("logits_ready")
        top_ready = [sem(f"top_ready{i}") for i in range(2)]
        hit_ready = [sem(f"hit_ready{i}") for i in range(2)]
        score_ready = [sem(f"score_ready{i}") for i in range(2)]
        best_ready = [sem(f"best_ready{i}") for i in range(2)]
        chosen = [sem(f"chosen{i}") for i in range(2)]
        rest_ready = sem("rest_ready")
        gap_ready = sem("gap_ready")
        expo_ready = sem("expo_ready")
        denom_ready = sem("denom_ready")
        inv_ready = sem("inv_ready")
        weight_ready = [sem(f"weight_ready{i}") for i in range(2)]
        part_ready = sem("part_ready")
        gates_ready = sem("gates_ready")
        gh_ready = sem("gh_ready")
        g_turned = sem("g_turned")
        g_hi_done = sem("g_hi_done")
        g_lo_done = sem("g_lo_done")
        out_product = sem("out_product")
        x_staged = sem("x_staged")
        stage_free = [sem(f"stage_free{s}") for s in range(STAGES)]

        block = ctx.enter_context(nc.Block())

        @block.sync
        def _(sp):
            dram = {"A": a} | {f"W{d}": w_blocks[d] for d in range(GROUP)}
            dram |= {f"F{h}{q}": ffn_w[h, q] for h in range(NH) for q in range(KD // 2)}

            def load_low_rank(h):
                sp.dma_start(stage[:, AF_STAGE[h], :], lora_a[:, halves[h]]).then_inc(af_loaded[h], 16)
                if h == 0:
                    sp.dma_start(coef[:, :], lora_weights.rearrange("(e a) -> e a", a=1)
                                 .unsqueeze(1).to_broadcast([E, R, 1])).then_inc(coef_loaded, 16)
                sp.dma_start(stage[:, BF_STAGE[h], :], lora_b[:, halves[h]]).then_inc(bf_loaded[h], 16)

            ended = {"F03": [(ft0_even_lo, 1), (ft0_odd_lo, 1)], "W1": [(w_lo_done, 1), (w0_front_lo, 1)],
                     "W2": [(ft0_even_lo, 2), (ft0_odd_lo, 2)], "F10": [(ft0_even_lo, 3), (ft0_odd_lo, 3)],
                     "F11": [(ft0_even_lo, 4), (ft0_odd_lo, 4)], "F12": [(w_lo_done, 2)], "F13": [(w_lo_done, 3)],
                     "A": [(ft1_lo, 2)]}
            load_low_rank(0)
            for name, slot in PIECES:
                for s, count in ended.get(name, []):
                    sp.wait_ge(s, count)
                sp.dma_start(raw[:, slot, :], dram[name]).then_inc(raw_loaded[slot], 16)
                if name == "F00":
                    load_low_rank(1)
            sp.dma_start(wr_raw[:, :, :], wr).then_inc(wr_loaded, 16)
            for b in range(P // SEQ):
                sp.dma_start(ids_raw[SEQ * b:SEQ * (b + 1), :], ids[b, :].partition_broadcast(SEQ))\
                  .then_inc(ids_loaded, 16)
            sp.dma_start(bias_col[:, :], bias).then_inc(bias_loaded, 16)
            for d in range(GROUP, KM):
                if d < 2 * GROUP:
                    sp.wait_ge(ft1_lo, 2 * (d - GROUP) + 4)
                else:
                    sp.wait_ge(w_lo_done, d - GROUP + 1)
                sp.dma_start(raw[:, d % GROUP, :], w_blocks[d]).then_inc(raw_loaded[d % GROUP], 16)

            def load_x(t, used):
                for i in range(4):
                    sp.wait_ge(*used(i))
                    sp.dma_start(raw[:, X_SLOT[i], :], x[bass.ds(4 * t + i, 1), :, :]
                                 .rearrange("a p n -> (a p) n")).then_inc(raw_loaded[X_SLOT[i]], 16)

            def store(t):
                for ob in range(KD):
                    sp.wait_ge(bank_read, M_BLOCKS + KD * t + ob + 1)
                    sp.dma_start(out[bass.ds(KD * t + ob, 1), :, :].rearrange("a p n -> (a p) n"),
                                 stage[:, ob % STAGES, :]).then_inc(stage_free[ob % STAGES], 16)

            load_x(0, lambda i: (aw_lo_done, 2) if i == 0 else (w_lo_done, KM - GROUP + i))
            with sp.Fori(0, TILES - 1) as t:
                load_x(t + 1, lambda i: (x_lo_done, 4 * t + i + 1))
                store(t)
            store(TILES - 1)
            for s in range(STAGES):
                sp.wait_ge(stage_free[s], 16 + 16 * TILES * KD // STAGES)

        @block.scalar
        def _(act):
            def hi_af(h):
                act.wait_ge(af_loaded[h], 16)
                nc.scalar.activation(af_hi[:, halves[h]], stage[:, AF_STAGE[h], :], ACT.Copy).then_inc(af_hi_done, 1)

            def hi_bf(h):
                act.wait_ge(coef_loaded, 16)
                act.wait_ge(bf_loaded[h], 16)
                nc.scalar.activation(bf_hi[:, halves[h]], stage[:, BF_STAGE[h], :], ACT.Copy, scale=coef[:, 0:1])\
                  .then_inc(bf_hi_done, 1)

            def hi_ft(h, *chunks):
                for c in chunks:
                    half = halves[c % 2]
                    act.wait_ge(ft_added, KD * h + c + 1)
                    nc.scalar.activation(fx_hi[:, h, c, :], raw[:, slot_of[f"F{h}{c // 2}"], half],
                                         ACT.Copy).then_inc(ft_hi_done, 1)

            def hi_w(j, count):
                act.wait_ge(raw_loaded[slot_of[f"W{j}"] if isinstance(count, str) else j],
                            loaded[count] if isinstance(count, str) else count)
                nc.scalar.activation(w_hi[:, j, :, :].rearrange("p c n -> p (c n)"),
                                     raw[:, slot_of[f"W{j}"] if isinstance(count, str) else j, :],
                                     ACT.Copy).then_inc(w_hi_done, 1)

            def hi_m(n, d, h, b):
                act.wait_ge(m_product, n + 1)
                nc.scalar.activation(m_hi[:, bass.ds(d, 1), h * HALF:(h + 1) * HALF].rearrange("p a n -> p (a n)"),
                                     ps[:, b, :], ACT.Copy).then_inc(m_hi_done, 1)

            def hi_x(t, i, parity):
                act.wait_ge(raw_loaded[X_SLOT[i]], 16 * FILLS_X[i] + 16 * (t + 1))
                dst = fx_hi[:, bass.ds(parity, 1), 2 * i:2 * i + 2, :].rearrange("p a c n -> p (a c n)")
                nc.scalar.activation(dst, raw[:, X_SLOT[i], :], ACT.Copy).then_inc(x_hi_done, 1)

            hi_af(0)
            hi_bf(0)
            hi_ft(0, 0)
            hi_af(1)
            hi_ft(0, 1)
            hi_bf(1)
            hi_w(0, "W0")
            hi_ft(0, 2, 3, 4, 5, 6, 7)
            hi_w(1, "W1")
            hi_w(2, "W2")
            hi_m(0, 0, 0, 0)
            hi_ft(1, 0, 1, 2, 3)
            hi_m(1, 1, 0, 1)
            hi_ft(1, 4, 5, 6, 7)
            hi_m(2, 2, 0, 2)
            act.wait_ge(raw_loaded[slot_of["A"]], loaded["A"])
            nc.scalar.activation(aw[:, :, 0:ER], raw[:, slot_of["A"], :].rearrange("p (c n) -> p c n", c=KD),
                                 ACT.Copy).then_inc(aw_hi_done, 1)
            act.wait_ge(wr_loaded, 16)
            nc.scalar.activation(aw[:, :, ER:HR], wr_raw[:, :, :], ACT.Copy).then_inc(aw_hi_done, 1)
            with act.Fori(1, GROUPS) as g:
                for j in range(GROUP):
                    hi_m(2 * GROUP * g - GROUP + j, GROUP * (g - 1) + j, 1, GROUP + j)
                    hi_w(j, 16 * fills[j] + 16 * g)
                for j in range(GROUP):
                    hi_m(2 * GROUP * g + j, GROUP * g + j, 0, j)
            for j in range(GROUP):
                for i in ((0, 1), (2,), (3,))[j]:
                    hi_x(0, i, 0)
                hi_m(M_BLOCKS - GROUP + j, KM - GROUP + j, 1, GROUP + j)

            def window(t):
                for s in range(SUBS):
                    act.wait_ge(h_product, SUBS * t + s + 1)
                    nc.scalar.activation(h_part[:, s, :], ps[:, C_BANK[s], HR:2 * HR], ACT.Copy)\
                      .then_inc(h_part_read, 1)
                act.wait_ge(gap_ready, t + 1)
                nc.scalar.activation(expo[:, :], gap[:, :], ACT.Exp).then_inc(expo_ready, 1)
                act.wait_ge(g_turned, t + 1)
                nc.scalar.activation(g_hi[:, :], ps[:, T_BANK, :], ACT.Copy).then_inc(g_hi_done, 1)

            with act.Fori(0, TILES - 1) as t:
                window(t)
                for i in range(4):
                    hi_x(t + 1, i, (t + 1) % 2)
            window(TILES - 1)

        @block.gpsimd
        def _(pool):
            def lo(dst, src, hi, hi_ready, count, done):
                pool.wait_ge(hi_ready, count)
                nc.gpsimd.tensor_tensor(dst, src, hi.bitcast(f32), ALU.subtract).then_inc(done, 1)

            def lo_ft(h, c, done):
                lo(fx_lo[:, h, c, :], raw[:, slot_of[f"F{h}{c // 2}"], halves[c % 2]], fx_hi[:, h, c, :],
                   ft_hi_done, KD * h + c + 1, done)

            def lo_w(j, slot, count, start=0):
                lo(w_lo[:, j, start:, :].rearrange("p c n -> p (c n)"), raw[:, slot, start * P:],
                   w_hi[:, j, start:, :].rearrange("p c n -> p (c n)"), w_hi_done, count, w_lo_done)

            for s in range(STAGES):
                pool.sem_inc(stage_free[s], 16)
            nc.gpsimd.memset(ident[:, :], 0.0).then_inc(ident_zero, 1)
            pool.wait_ge(ident_zero, 1)
            nc.gpsimd.affine_select(out=ident[:, :], in_=ident[:, :], compare_op=ALU.not_equal, fill=1.0,
                                    base=0, pattern=[[-1, P]], channel_multiplier=1).then_inc(ident_ready, 1)
            lo_ft(0, 0, ft0_even_lo)
            lo_w(0, slot_of["W0"], 1, start=KD // 2)
            for c in (2, 4, 6):
                lo_ft(0, c, ft0_even_lo)
            lo_w(1, slot_of["W1"], 2)
            lo_w(2, slot_of["W2"], 3)
            for c in range(KD):
                lo_ft(1, c, ft1_lo)
            lo(aw[:, :, HR:HR + ER], raw[:, slot_of["A"], :].rearrange("p (c n) -> p c n", c=KD), aw[:, :, 0:ER],
               aw_hi_done, 1, aw_lo_done)
            lo(aw[:, :, HR + ER:2 * HR], wr_raw[:, :, :], aw[:, :, ER:HR], aw_hi_done, 2, aw_lo_done)
            with pool.Fori(1, GROUPS) as g:
                for j in range(GROUP):
                    lo_w(j, j, GROUP * g + j + 1)

            with pool.Fori(0, TILES // 2) as pair:
                for par in range(2):
                    t = 2 * pair + par
                    for i in range(4):
                        lo(fx_lo[:, par, 2 * i:2 * i + 2, :].rearrange("p c n -> p (c n)"), raw[:, X_SLOT[i], :],
                           fx_hi[:, par, 2 * i:2 * i + 2, :].rearrange("p c n -> p (c n)"),
                           x_hi_done, 4 * t + i + 1, x_lo_done)
                    pool.wait_ge(x_lo_done, 4 * t + 4)
                    for ob in range(KD):
                        pool.wait_ge(stage_free[ob % STAGES], 16 * (KD // STAGES) * t + 16 * (ob // STAGES + 1))
                        nc.gpsimd.tensor_tensor(stage[:, ob % STAGES, :], fx_hi[:, par, ob, :].bitcast(f32),
                                                fx_lo[:, par, ob, :].bitcast(f32), ALU.add).then_inc(x_staged, 1)

        @block.vector
        def _(dve):
            mult, add, eq = ALU.mult, ALU.add, ALU.is_equal
            def lo_af(h):
                dve.wait_ge(af_hi_done, h + 1)
                nc.vector.tensor_tensor(af_lo[:, halves[h]], stage[:, AF_STAGE[h], :],
                                        af_hi[:, halves[h]].bitcast(f32), ALU.subtract).then_inc(af_lo_done, 1)

            def lo_bf(h):
                dve.wait_ge(bf_hi_done, h + 1)
                nc.vector.scalar_tensor_tensor(out=bf_lo[:, halves[h]], in0=stage[:, BF_STAGE[h], :],
                                               scalar=coef[:, 0:1], in1=bf_hi[:, halves[h]].bitcast(f32),
                                               op0=mult, op1=ALU.subtract).then_inc(bf_lo_done, 1)

            def add_ft(h, *chunks):
                for c in chunks:
                    piece = f"F{h}{c // 2}"
                    half = raw[:, slot_of[piece], halves[c % 2]]
                    dve.wait_ge(raw_loaded[slot_of[piece]], loaded[piece])
                    dve.wait_ge(ft_product, KD * h + c + 1)
                    nc.vector.scalar_tensor_tensor(out=half, in0=ps[:, FT_BANK[KD * h + c], :], scalar=SCALING,
                                                   in1=half, op0=mult, op1=add).then_inc(ft_added, 1)

            def lo_ft0(c):
                dve.wait_ge(ft_hi_done, c + 1)
                nc.vector.tensor_tensor(fx_lo[:, 0, c, :], raw[:, slot_of[f"F0{c // 2}"], halves[c % 2]],
                                        fx_hi[:, 0, c, :].bitcast(f32), ALU.subtract).then_inc(ft0_odd_lo, 1)

            def lo_m(n, d, h, b):
                cols = m_hi[:, bass.ds(d, 1), h * HALF:(h + 1) * HALF].rearrange("p a n -> p (a n)")
                dst = m_lo[:, bass.ds(d, 1), h * HALF:(h + 1) * HALF].rearrange("p a n -> p (a n)")
                dve.wait_ge(m_hi_done, n + 1)
                nc.vector.tensor_tensor(dst, ps[:, b, :], cols.bitcast(f32), ALU.subtract).then_inc(bank_read, 1)

            lo_af(0)
            lo_bf(0)
            add_ft(0, 0, 1)
            lo_af(1)
            lo_bf(1)
            lo_ft0(1)
            front = w_hi[:, 0, 0:KD // 2, :].rearrange("p c n -> p (c n)")
            dve.wait_ge(w_hi_done, 1)
            nc.vector.tensor_tensor(w_lo[:, 0, 0:KD // 2, :].rearrange("p c n -> p (c n)"),
                                    raw[:, slot_of["W0"], 0:KD // 2 * P], front.bitcast(f32), ALU.subtract)\
              .then_inc(w0_front_lo, 1)
            for c in (2, 4, 6):
                add_ft(0, c, c + 1)
                lo_ft0(c + 1)
            lo_m(0, 0, 0, 0)
            add_ft(1, 0, 1, 2, 3)
            lo_m(1, 1, 0, 1)
            add_ft(1, 4, 5, 6, 7)
            lo_m(2, 2, 0, 2)
            for e in range(E):
                ins = nc.vector.memset(rank[:, :, e:e + 1], float(E - e))
            ins.then_inc(rank_ready, 1)
            dve.wait_ge(ids_loaded, 16 * P // SEQ)
            nc.vector.tensor_scalar(ids_rank[:, :], ids_raw[:, :], -1.0, float(E), mult, add).then_inc(ids_ready, 1)
            dve.wait_ge(rank_ready, 1)
            dve.wait_ge(ids_ready, 1)
            nc.vector.tensor_tensor(lang[:, :, :], rank[:, :, :],
                                    ids_rank[:, :].unsqueeze(2).to_broadcast([P, ROWS // P, E]), eq)\
              .then_inc(lang_hit, 1)
            dve.wait_ge(lang_hit, 1)
            nc.vector.tensor_scalar(lang[:, :, :], lang[:, :, :], LANG_BIAS, None, mult).then_inc(lang_ready, 1)
            with dve.Fori(1, GROUPS) as g:
                for j in range(GROUP):
                    lo_m(2 * GROUP * g - GROUP + j, GROUP * (g - 1) + j, 1, GROUP + j)
                for j in range(GROUP):
                    lo_m(2 * GROUP * g + j, GROUP * g + j, 0, j)
            for j in range(GROUP):
                lo_m(M_BLOCKS - GROUP + j, KM - GROUP + j, 1, GROUP + j)
            dve.wait_ge(lang_ready, 1)
            dve.wait_ge(bias_loaded, 16)

            def spread(v):
                return v.unsqueeze(2).to_broadcast([P, SUBS, E])

            def choose(t, i, src):
                nc.vector.tensor_reduce(top[:, i, :], src[:, :, :], AX.X, ALU.max).then_inc(top_ready[i], 1)
                dve.wait_ge(top_ready[i], t + 1)
                nc.vector.tensor_tensor(hit[:, i, :, :], src[:, :, :], spread(top[:, i, :]), eq)\
                  .then_inc(hit_ready[i], 1)
                dve.wait_ge(hit_ready[i], t + 1)
                nc.vector.tensor_tensor(score[:, i, :, :], hit[:, i, :, :], rank[:, 0:SUBS, :], mult)\
                  .then_inc(score_ready[i], 1)
                dve.wait_ge(score_ready[i], t + 1)
                nc.vector.tensor_reduce(best[:, i, :], score[:, i, :, :], AX.X, ALU.max).then_inc(best_ready[i], 1)
                dve.wait_ge(best_ready[i], t + 1)
                nc.vector.tensor_tensor((first, second)[i][:, :, :], score[:, i, :, :], spread(best[:, i, :]), eq)\
                  .then_inc(chosen[i], 1)
                dve.wait_ge(chosen[i], t + 1)

            def window(t):
                for s in range(SUBS):
                    dve.wait_ge(h_part_read, SUBS * t + s + 1)
                    nc.vector.tensor_tensor(hl[:, s, :], ps[:, C_BANK[s], 0:HR], h_part[:, s, :], add)\
                      .then_inc(hl_ready, 1)
                dve.wait_ge(hl_ready, SUBS * t + SUBS)
                nc.vector.tensor_tensor(logits[:, :, :], hl[:, :, ER:HR], lang[:, bass.ds(SUBS * t, SUBS), :], add)\
                  .then_inc(logits_ready, 1)
                dve.wait_ge(logits_ready, t + 1)
                choose(t, 0, logits)
                nc.vector.scalar_tensor_tensor(out=rest[:, :, :], in0=first[:, :, :], scalar=BELOW,
                                               in1=logits[:, :, :], op0=mult, op1=add).then_inc(rest_ready, 1)
                dve.wait_ge(rest_ready, t + 1)
                choose(t, 1, rest)
                nc.vector.tensor_tensor(gap[:, :], top[:, 1, :], top[:, 0, :], ALU.subtract).then_inc(gap_ready, 1)
                dve.wait_ge(expo_ready, t + 1)
                nc.vector.tensor_scalar(denom[:, :], expo[:, :], 1.0, None, add).then_inc(denom_ready, 1)
                dve.wait_ge(denom_ready, t + 1)
                nc.vector.reciprocal(inv[:, :], denom[:, :]).then_inc(inv_ready, 1)
                dve.wait_ge(inv_ready, t + 1)
                nc.vector.tensor_scalar(weight[:, 0, :], inv[:, :], SCALING, None, mult).then_inc(weight_ready[0], 1)
                dve.wait_ge(weight_ready[0], t + 1)
                nc.vector.tensor_tensor(weight[:, 1, :], expo[:, :], weight[:, 0, :], mult)\
                  .then_inc(weight_ready[1], 1)
                dve.wait_ge(weight_ready[1], t + 1)
                for i in range(2):
                    ins = nc.vector.tensor_tensor(part[:, i, :, :], (first, second)[i][:, :, :],
                                                  spread(weight[:, i, :]), mult)
                ins.then_inc(part_ready, 1)
                dve.wait_ge(part_ready, t + 1)
                nc.vector.tensor_tensor(gates[:, :, :], part[:, 0, :, :], part[:, 1, :, :], add)\
                  .then_inc(gates_ready, 1)
                dve.wait_ge(gates_ready, t + 1)
                for s in range(SUBS):
                    ins = nc.vector.tensor_tensor(
                        gh[:, s, :].rearrange("p (e r) -> p e r", r=R),
                        hl[:, s, 0:ER].rearrange("p (e r) -> p e r", r=R),
                        gates[:, s, :].unsqueeze(2).to_broadcast([P, E, R]), mult)
                ins.then_inc(gh_ready, 1)
                dve.wait_ge(g_hi_done, t + 1)
                nc.vector.tensor_tensor(g_lo[:, :], ps[:, T_BANK, :], g_hi[:, :].bitcast(f32), ALU.subtract)\
                  .then_inc(g_lo_done, 1)
                for ob in range(KD):
                    dve.wait_ge(out_product, KD * t + ob + 1)
                    dve.wait_ge(x_staged, KD * t + ob + 1)
                    st = stage[:, ob % STAGES, :]
                    nc.vector.scalar_tensor_tensor(out=st, in0=ps[:, ob % 4, :], scalar=bias_col[:, ob:ob + 1],
                                                   in1=st, op0=add, op1=add).then_inc(bank_read, 1)

            with dve.Fori(0, TILES) as t:
                window(t)

        @block.tensor
        def _(pe):
            def ft(h, *chunks):
                for c in chunks:
                    n = KD * h + c
                    before = [m for m in range(n) if FT_BANK[m] == FT_BANK[n]]
                    if before:
                        pe.wait_ge(ft_added, before[-1] + 1)
                    cols, dst = slice(c * P, (c + 1) * P), ps[:, FT_BANK[n], :]
                    pe.wait_ge(bf_hi_done, h + 1)
                    pe.wait_ge(af_hi_done, c // 4 + 1)
                    nc.tensor.matmul(dst, af_hi[:, cols], bf_hi[:, halves[h]], start=True, stop=False)
                    pe.wait_ge(af_lo_done, c // 4 + 1)
                    nc.tensor.matmul(dst, af_lo[:, cols], bf_hi[:, halves[h]], start=False, stop=False)
                    pe.wait_ge(bf_lo_done, h + 1)
                    nc.tensor.matmul(dst, af_hi[:, cols], bf_lo[:, halves[h]], start=False, stop=True)\
                      .then_inc(ft_product, 1)

            def m_block(j, h, b, arriving=False):
                for c in range(KD):
                    if arriving and h == 0:
                        pe.wait_ge(ft0_odd_lo if c % 2 else ft0_even_lo, c // 2 + 1)
                        if c % (KD // 2) == 0:
                            pe.wait_ge(w_lo_done if c else w0_front_lo, 1)
                    if arriving and h == 1:
                        pe.wait_ge(ft1_lo, c + 1)
                    nc.tensor.matmul(ps[:, b, :], w_lo[:, j, c, :], fx_hi[:, h, c, :], start=(c == 0), stop=False)
                    nc.tensor.matmul(ps[:, b, :], w_hi[:, j, c, :], fx_lo[:, h, c, :], start=False, stop=False)
                for c in range(KD):
                    ins = nc.tensor.matmul(ps[:, b, :], w_hi[:, j, c, :], fx_hi[:, h, c, :],
                                           start=False, stop=(c == KD - 1))
                ins.then_inc(m_product, 1)

            pe.wait_ge(ident_ready, 1)
            for _ in range(WARM_UP):
                nc.tensor.matmul(ps[:, 7, 0:P], ident[:, :], ident[:, :], start=True, stop=True)
            ft(0, *range(KD))
            ft(1, 0, 1, 2)
            m_block(0, 0, 0, arriving=True)
            ft(1, 3)
            pe.wait_ge(ft_added, KD)
            pe.wait_ge(w_lo_done, 2)
            m_block(1, 0, 1)
            ft(1, *range(4, KD))
            pe.wait_ge(w_lo_done, 3)
            m_block(2, 0, 2)
            pe.wait_ge(ft_added, NH * KD)
            for j in range(GROUP):
                m_block(j, 1, GROUP + j, arriving=(j == 0))
            with pe.Fori(1, GROUPS) as g:
                for h in range(NH):
                    for j in range(GROUP):
                        if h == 0:
                            pe.wait_ge(w_lo_done, GROUP * g + j + 1)
                        pe.wait_ge(bank_read, 2 * GROUP * (g - 1) + GROUP * h + j + 1)
                        m_block(j, h, GROUP * h + j)

            def h_and_logits(t, par):
                for s in range(SUBS):
                    rows, dst = slice(s * P, (s + 1) * P), ps[:, C_BANK[s], 0:2 * HR]
                    if s == 2:
                        pe.wait_ge(bank_read, M_BLOCKS)
                    for c in range(KD):
                        if s == 0 and c % 2 == 0:
                            pe.wait_ge(x_lo_done, 4 * t + c // 2 + 1)
                        nc.tensor.matmul(dst, fx_hi[:, par, c, rows], aw[:, c, :], start=(c == 0), stop=False)
                        ins = nc.tensor.matmul(dst[:, HR:2 * HR], fx_lo[:, par, c, rows], aw[:, c, 0:HR],
                                               start=False, stop=(c == KD - 1))
                    ins.then_inc(h_product, 1)

            def features(t, ob, par):
                cols, dst = slice(ob * P, (ob + 1) * P), ps[:, ob % 4, :]
                pe.wait_ge(bank_read, M_BLOCKS - 3 + KD * t + ob)
                for c in range(KD):
                    nc.tensor.matmul(dst, m_lo[:, c, cols], fx_hi[:, par, c, :], start=(c == 0), stop=False)
                    nc.tensor.matmul(dst, m_hi[:, c, cols], fx_lo[:, par, c, :], start=False, stop=False)
                for c in range(KD):
                    nc.tensor.matmul(dst, m_hi[:, c, cols], fx_hi[:, par, c, :], start=False, stop=False)

            def turn(t):
                pe.wait_ge(gh_ready, t + 1)
                for s in range(SUBS):
                    ins = nc.tensor.transpose(ps[:, T_BANK, s * P:(s + 1) * P], gh[:, s, :], ident[:, :])
                ins.then_inc(g_turned, 1)

            def ranks(ob):
                cols, dst = slice(ob * P, (ob + 1) * P), ps[:, ob % 4, :]
                nc.tensor.matmul(dst, m_lo[:, KD, cols], g_hi[:, :], start=False, stop=False)
                nc.tensor.matmul(dst, m_hi[:, KD, cols], g_lo[:, :], start=False, stop=False)
                nc.tensor.matmul(dst, m_hi[:, KD, cols], g_hi[:, :], start=False, stop=True)\
                  .then_inc(out_product, 1)

            pe.wait_ge(aw_lo_done, 2)
            with pe.Fori(0, TILES // 2) as pair:
                for par in range(2):
                    t = 2 * pair + par
                    h_and_logits(t, par)
                    for ob in range(KD):
                        features(t, ob, par)
                        if ob == 1:
                            turn(t)
                        if ob == 2:
                            pe.wait_ge(g_lo_done, t + 1)
                            ranks(0)
                            ranks(1)
                        if ob >= 2:
                            ranks(ob)


def kernel(x, itok_B_0_7, L0_cond_W, L0_cond_Wr, L0_cond_A, L0_cond_B, L0_ffn_lora_A, L0_ffn_lora_B, L0_ffn_W,
           L0_ffn_bias, L0_ffn_lora_weights):
    import numpy as np
    import concourse.bacc as bacc
    from concourse.bass_utils import run_bass_kernel_spmd

    n = np.asarray
    xt = n(x).reshape(TILES, TILE, KD // 2, 2, P).transpose(0, 2, 4, 3, 1).reshape(-1, P, 1024)
    w = n(L0_cond_W).reshape(KD, P, KD, P).transpose(2, 1, 0, 3).reshape(KD, P, 1024)
    b = n(L0_cond_B).transpose(1, 0, 2).reshape(KD, P, ER).transpose(1, 0, 2).reshape(1, P, 1024)
    arrays = {
        "x": xt,
        "ids": n(itok_B_0_7).reshape(-1, P // SEQ).T,
        "w_blocks": np.concatenate([w, b]),
        "wr": n(L0_cond_Wr).reshape(E, KD, P).transpose(2, 1, 0),
        "a": n(L0_cond_A).reshape(ER, KD, P).transpose(2, 1, 0).reshape(P, 1024),
        "lora_a": n(L0_ffn_lora_A).reshape(ER, D),
        "lora_b": n(L0_ffn_lora_B).transpose(0, 2, 1).reshape(ER, D),
        "ffn_w": n(L0_ffn_W).reshape(NH, HALF, KD // 2, 2, P).transpose(0, 2, 4, 3, 1).reshape(NH, KD // 2, P, 1024),
        "bias": n(L0_ffn_bias).reshape(KD, P).T,
        "lora_weights": n(L0_ffn_lora_weights),
    }
    nc = bacc.Bacc("TRN2", target_bir_lowering=False, num_devices=1)
    args, given = [], {}
    for name, v in arrays.items():
        v = np.ascontiguousarray(v)
        given[f"in_{name}"] = v
        args.append(nc.dram_tensor(f"in_{name}", v.shape, mybir.dt.from_np(v.dtype), kind="ExternalInput").ap())
    args.append(nc.dram_tensor("out_t", (TILES * KD, P, TILE), mybir.dt.float32, kind="ExternalOutput").ap())
    adaln_ffn(nc, *args)
    got = run_bass_kernel_spmd(nc, [given], core_ids=[0]).results[0]["out_t"]
    return got.reshape(TILES, KD, P, TILE).transpose(0, 3, 1, 2).reshape(n(x).shape)
```

```python
import concourse.bass as bass
from concourse import mybir
from contextlib import ExitStack



ROWS, D = 2048, 1024
P = 128
KD = D // P
E, R = 8, 16
ER = E * R
HALF = 512
NH = D // HALF
TILE = 512
TILES = ROWS // TILE
SUBS = TILE // P
SEQ = 64
KM = KD + 1
GROUP = 3
GROUPS = KM // GROUP
HR = ER + E
LANG_BIAS = 5.0
SCALING = 2.0
BELOW = -3.0e38
RAW = 4
STAGES = 4
C_BANK = [6, 7, 4, 5]
T_BANK = 6
FT_BANK = [4, 5, 6, 7, 1, 2, 3, 4, 5, 6, 7, 1, 4, 5, 6, 7]
M_BANK0 = [0, 2, 1]
WARM_UP = 8

PIECES = [("F00", 0), ("W0", 1), ("F01", 2), ("F02", 3), ("F03", 0), ("W1", 1), ("W2", 2),
          ("F10", 3), ("F11", 0), ("F12", 1), ("F13", 2), ("A", 3)]
X_SLOT = [3, 0, 1, 2]


def adaln_ffn(nc, x, ids, w_blocks, wr, a, lora_a, lora_b, ffn_w, bias, lora_weights, out):
    f32, f32r, i32 = mybir.dt.float32, mybir.dt.float32r, mybir.dt.int32
    ALU = mybir.AluOpType
    ACT = mybir.ActivationFunctionType
    AX = mybir.AxisListType

    slot_of, loaded = {}, {}
    fills = [0] * RAW
    for name, slot in PIECES:
        fills[slot] += 1
        slot_of[name], loaded[name] = slot, 16 * fills[slot]
    FILLS_X = [fills[s] + (GROUPS - 1) * (s < GROUP) for s in X_SLOT]
    M_BLOCKS = KM * NH

    ctx = ExitStack()
    with ctx:
        def sb(name, shape, dt=f32):
            return ctx.enter_context(nc.sbuf_tensor(name, shape, dt))

        def sem(name):
            return ctx.enter_context(nc.semaphore(name))

        raw = sb("raw", [P, RAW, 1024])
        m_hi = sb("m_hi", [P, KM, D], f32r)
        m_lo = sb("m_lo", [P, KM, D], f32r)
        fx_hi = sb("fx_hi", [P, 2, KD, 512], f32r)
        fx_lo = sb("fx_lo", [P, 2, KD, 512], f32r)
        w_hi = sb("w_hi", [P, GROUP, KD, P], f32r)
        w_lo = sb("w_lo", [P, GROUP, KD, P], f32r)
        aw = sb("aw", [P, KD, 2 * HR], f32r)
        wr_raw = sb("wr_raw", [P, KD, E])
        g_hi = sb("g_hi", [P, TILE], f32r)
        g_lo = sb("g_lo", [P, TILE], f32r)
        stage = sb("stage", [P, STAGES, TILE])
        h_part = sb("h_part", [P, SUBS, HR])
        hl = sb("hl", [P, SUBS, HR])
        gh = sb("gh", [P, SUBS, ER])
        ident = sb("ident", [P, P])
        coef = sb("coef", [P, 1])
        bias_col = sb("bias_col", [P, KD])
        ids_raw = sb("ids_raw", [P, ROWS // P], i32)
        ids_rank = sb("ids_rank", [P, ROWS // P])
        rank = sb("rank", [P, ROWS // P, E])
        lang = sb("lang", [P, ROWS // P, E])
        logits = sb("logits", [P, SUBS, E])
        rest = sb("rest", [P, SUBS, E])
        hit = sb("hit", [P, 2, SUBS, E])
        score = sb("score", [P, 2, SUBS, E])
        best = sb("best", [P, 2, SUBS])
        top = sb("top", [P, 2, SUBS])
        first = sb("first", [P, SUBS, E])
        second = sb("second", [P, SUBS, E])
        gap = sb("gap", [P, SUBS])
        expo = sb("expo", [P, SUBS])
        denom = sb("denom", [P, SUBS])
        inv = sb("inv", [P, SUBS])
        weight = sb("weight", [P, 2, SUBS])
        part = sb("part", [P, 2, SUBS, E])
        gates = sb("gates", [P, SUBS, E])

        ps = ctx.enter_context(nc.psum_tensor("ps", [P, 8, 512], f32))

        af_hi, af_lo = m_hi[:, KM - 1, :], m_lo[:, KM - 1, :]
        bf_hi, bf_lo = m_hi[:, KM - 2, :], m_lo[:, KM - 2, :]
        AF_STAGE, BF_STAGE = [0, 2], [1, 3]
        halves = [slice(h * HALF, (h + 1) * HALF) for h in range(NH)]

        raw_loaded = [sem(f"raw_loaded{s}") for s in range(RAW)]
        af_loaded = [sem(f"af_loaded{h}") for h in range(NH)]
        bf_loaded = [sem(f"bf_loaded{h}") for h in range(NH)]
        coef_loaded = sem("coef_loaded")
        wr_loaded = sem("wr_loaded")
        ids_loaded = sem("ids_loaded")
        bias_loaded = sem("bias_loaded")
        af_hi_done, af_lo_done = sem("af_hi_done"), sem("af_lo_done")
        bf_hi_done, bf_lo_done = sem("bf_hi_done"), sem("bf_lo_done")
        ft_hi_done = sem("ft_hi_done")
        ft0_even_lo = sem("ft0_even_lo")
        ft0_odd_lo = sem("ft0_odd_lo")
        ft1_lo = sem("ft1_lo")
        w_hi_done, w_lo_done = sem("w_hi_done"), sem("w_lo_done")
        w_front_lo = sem("w_front_lo")
        aw_hi_done, aw_lo_done = sem("aw_hi_done"), sem("aw_lo_done")
        x_hi_done, x_lo_done = sem("x_hi_done"), sem("x_lo_done")
        ft_product = sem("ft_product")
        ft_added = sem("ft_added")
        m_product = sem("m_product")
        m_hi_done = sem("m_hi_done")
        bank_read = sem("bank_read")
        ident_zero = sem("ident_zero")
        ident_ready = sem("ident_ready")
        rank_ready = sem("rank_ready")
        ids_ready = sem("ids_ready")
        lang_hit = sem("lang_hit")
        lang_ready = sem("lang_ready")
        h_product = sem("h_product")
        h_part_read = sem("h_part_read")
        hl_ready = sem("hl_ready")
        logits_ready = sem("logits_ready")
        top_ready = [sem(f"top_ready{i}") for i in range(2)]
        hit_ready = [sem(f"hit_ready{i}") for i in range(2)]
        score_ready = [sem(f"score_ready{i}") for i in range(2)]
        best_ready = [sem(f"best_ready{i}") for i in range(2)]
        chosen = [sem(f"chosen{i}") for i in range(2)]
        rest_ready = sem("rest_ready")
        gap_ready = sem("gap_ready")
        expo_ready = sem("expo_ready")
        denom_ready = sem("denom_ready")
        inv_ready = sem("inv_ready")
        weight_ready = [sem(f"weight_ready{i}") for i in range(2)]
        part_ready = sem("part_ready")
        gates_ready = sem("gates_ready")
        gh_ready = sem("gh_ready")
        g_turned = sem("g_turned")
        g_hi_done = sem("g_hi_done")
        g_lo_done = sem("g_lo_done")
        out_product = sem("out_product")
        x_staged = sem("x_staged")
        stage_free = [sem(f"stage_free{s}") for s in range(STAGES)]

        block = ctx.enter_context(nc.Block())

        @block.sync
        def _(sp):
            dram = {"A": a} | {f"W{d}": w_blocks[d] for d in range(GROUP)}
            dram |= {f"F{h}{q}": ffn_w[h, q] for h in range(NH) for q in range(KD // 2)}

            def load_low_rank(h):
                sp.dma_start(stage[:, AF_STAGE[h], :], lora_a[:, halves[h]]).then_inc(af_loaded[h], 16)
                sp.dma_start(stage[:, BF_STAGE[h], :], lora_b[:, halves[h]]).then_inc(bf_loaded[h], 16)
                if h == 0:
                    sp.dma_start(coef[:, :], lora_weights.rearrange("(e a) -> e a", a=1)
                                 .unsqueeze(1).to_broadcast([E, R, 1])).then_inc(coef_loaded, 16)

            ended = {"F03": [(ft0_even_lo, 1), (ft0_odd_lo, 1)], "W1": [(w_lo_done, 1), (w_front_lo, 1)],
                     "W2": [(ft0_even_lo, 2), (ft0_odd_lo, 2)], "F10": [(ft0_even_lo, 3), (ft0_odd_lo, 3)],
                     "F11": [(ft0_even_lo, 4), (ft0_odd_lo, 4)], "F12": [(w_lo_done, 2), (w_front_lo, 2)],
                     "F13": [(w_lo_done, 3)], "A": [(ft1_lo, 2)]}
            load_low_rank(0)
            for name, slot in PIECES:
                for s, count in ended.get(name, []):
                    sp.wait_ge(s, count)
                sp.dma_start(raw[:, slot, :], dram[name]).then_inc(raw_loaded[slot], 16)
                if name == "F00":
                    load_low_rank(1)
            sp.dma_start(wr_raw[:, :, :], wr).then_inc(wr_loaded, 16)
            for b in range(P // SEQ):
                sp.dma_start(ids_raw[SEQ * b:SEQ * (b + 1), :], ids[b, :].partition_broadcast(SEQ))\
                  .then_inc(ids_loaded, 16)
            sp.dma_start(bias_col[:, :], bias).then_inc(bias_loaded, 16)
            for d in range(GROUP, KM):
                if d < 2 * GROUP:
                    sp.wait_ge(ft1_lo, 2 * (d - GROUP) + 4)
                else:
                    sp.wait_ge(w_lo_done, d - GROUP + 1)
                sp.dma_start(raw[:, d % GROUP, :], w_blocks[d]).then_inc(raw_loaded[d % GROUP], 16)

            def load_x(t, used):
                for i in range(4):
                    sp.wait_ge(*used(i))
                    sp.dma_start(raw[:, X_SLOT[i], :], x[bass.ds(4 * t + i, 1), :, :]
                                 .rearrange("a p n -> (a p) n")).then_inc(raw_loaded[X_SLOT[i]], 16)

            def store(t):
                for ob in range(KD):
                    sp.wait_ge(bank_read, M_BLOCKS + KD * t + ob + 1)
                    sp.dma_start(out[bass.ds(KD * t + ob, 1), :, :].rearrange("a p n -> (a p) n"),
                                 stage[:, ob % STAGES, :]).then_inc(stage_free[ob % STAGES], 16)

            load_x(0, lambda i: (aw_lo_done, 2) if i == 0 else (w_lo_done, KM - GROUP + i))
            with sp.Fori(0, TILES - 1) as t:
                load_x(t + 1, lambda i: (x_lo_done, 4 * t + i + 1))
                store(t)
            store(TILES - 1)
            for s in range(STAGES):
                sp.wait_ge(stage_free[s], 16 + 16 * TILES * KD // STAGES)

        @block.scalar
        def _(act):
            def hi_af(h):
                act.wait_ge(af_loaded[h], 16)
                nc.scalar.activation(af_hi[:, halves[h]], stage[:, AF_STAGE[h], :], ACT.Copy).then_inc(af_hi_done, 1)

            def hi_bf(h):
                act.wait_ge(coef_loaded, 16)
                act.wait_ge(bf_loaded[h], 16)
                nc.scalar.activation(bf_hi[:, halves[h]], stage[:, BF_STAGE[h], :], ACT.Copy, scale=coef[:, 0:1])\
                  .then_inc(bf_hi_done, 1)

            def hi_ft(h, *chunks):
                for c in chunks:
                    half = halves[c % 2]
                    act.wait_ge(ft_added, KD * h + c + 1)
                    nc.scalar.activation(fx_hi[:, h, c, :], raw[:, slot_of[f"F{h}{c // 2}"], half],
                                         ACT.Copy).then_inc(ft_hi_done, 1)

            def hi_w(j, slot, count):
                act.wait_ge(raw_loaded[slot], count)
                nc.scalar.activation(w_hi[:, j, :, :].rearrange("p c n -> p (c n)"), raw[:, slot, :],
                                     ACT.Copy).then_inc(w_hi_done, 1)

            def hi_m(n, d, h, b):
                act.wait_ge(m_product, n + 1)
                nc.scalar.activation(m_hi[:, bass.ds(d, 1), h * HALF:(h + 1) * HALF].rearrange("p a n -> p (a n)"),
                                     ps[:, b, :], ACT.Copy).then_inc(m_hi_done, 1)

            def hi_x(t, i, parity):
                act.wait_ge(raw_loaded[X_SLOT[i]], 16 * FILLS_X[i] + 16 * (t + 1))
                dst = fx_hi[:, bass.ds(parity, 1), 2 * i:2 * i + 2, :].rearrange("p a c n -> p (a c n)")
                nc.scalar.activation(dst, raw[:, X_SLOT[i], :], ACT.Copy).then_inc(x_hi_done, 1)

            hi_af(0)
            hi_bf(0)
            hi_af(1)
            hi_ft(0, 0, 1)
            hi_bf(1)
            hi_w(0, slot_of["W0"], loaded["W0"])
            hi_ft(0, 2, 3, 4, 5, 6, 7)
            hi_w(1, slot_of["W1"], loaded["W1"])
            hi_w(2, slot_of["W2"], loaded["W2"])
            hi_m(0, 0, 0, M_BANK0[0])
            hi_ft(1, 0, 1, 2, 3)
            hi_m(1, 1, 0, M_BANK0[1])
            hi_ft(1, 4, 5, 6, 7)
            hi_m(2, 2, 0, M_BANK0[2])
            act.wait_ge(raw_loaded[slot_of["A"]], loaded["A"])
            nc.scalar.activation(aw[:, :, 0:ER], raw[:, slot_of["A"], :].rearrange("p (c n) -> p c n", c=KD),
                                 ACT.Copy).then_inc(aw_hi_done, 1)
            act.wait_ge(wr_loaded, 16)
            nc.scalar.activation(aw[:, :, ER:HR], wr_raw[:, :, :], ACT.Copy).then_inc(aw_hi_done, 1)
            with act.Fori(1, GROUPS) as g:
                for j in range(GROUP):
                    hi_m(2 * GROUP * g - GROUP + j, GROUP * (g - 1) + j, 1, GROUP + j)
                    hi_w(j, j, 16 * fills[j] + 16 * g)
                for j in range(GROUP):
                    hi_m(2 * GROUP * g + j, GROUP * g + j, 0, j)
            for j in range(GROUP):
                for i in ((0, 1), (2,), (3,))[j]:
                    hi_x(0, i, 0)
                hi_m(M_BLOCKS - GROUP + j, KM - GROUP + j, 1, GROUP + j)

            def window(t):
                for s in range(SUBS):
                    act.wait_ge(h_product, SUBS * t + s + 1)
                    nc.scalar.activation(h_part[:, s, :], ps[:, C_BANK[s], HR:2 * HR], ACT.Copy)\
                      .then_inc(h_part_read, 1)
                act.wait_ge(gap_ready, t + 1)
                nc.scalar.activation(expo[:, :], gap[:, :], ACT.Exp).then_inc(expo_ready, 1)
                act.wait_ge(g_turned, t + 1)
                nc.scalar.activation(g_hi[:, :], ps[:, T_BANK, :], ACT.Copy).then_inc(g_hi_done, 1)

            with act.Fori(0, TILES - 1) as t:
                window(t)
                for i in range(4):
                    hi_x(t + 1, i, (t + 1) % 2)
            window(TILES - 1)

        @block.gpsimd
        def _(pool):
            def lo(dst, src, hi, hi_ready, count, done):
                pool.wait_ge(hi_ready, count)
                nc.gpsimd.tensor_tensor(dst, src, hi.bitcast(f32), ALU.subtract).then_inc(done, 1)

            def lo_ft(h, c, done):
                lo(fx_lo[:, h, c, :], raw[:, slot_of[f"F{h}{c // 2}"], halves[c % 2]], fx_hi[:, h, c, :],
                   ft_hi_done, KD * h + c + 1, done)

            def lo_w(j, slot, count, start=0):
                lo(w_lo[:, j, start:, :].rearrange("p c n -> p (c n)"), raw[:, slot, start * P:],
                   w_hi[:, j, start:, :].rearrange("p c n -> p (c n)"), w_hi_done, count, w_lo_done)

            for s in range(STAGES):
                pool.sem_inc(stage_free[s], 16)
            nc.gpsimd.memset(ident[:, :], 0.0).then_inc(ident_zero, 1)
            pool.wait_ge(ident_zero, 1)
            nc.gpsimd.affine_select(out=ident[:, :], in_=ident[:, :], compare_op=ALU.not_equal, fill=1.0,
                                    base=0, pattern=[[-1, P]], channel_multiplier=1).then_inc(ident_ready, 1)
            lo_ft(0, 0, ft0_even_lo)
            lo_w(0, slot_of["W0"], 1, start=KD // 2)
            for c in (2, 4, 6):
                lo_ft(0, c, ft0_even_lo)
            lo_w(1, slot_of["W1"], 2, start=KD // 2)
            lo_w(2, slot_of["W2"], 3)
            for c in range(KD):
                lo_ft(1, c, ft1_lo)
            lo(aw[:, :, HR:HR + ER], raw[:, slot_of["A"], :].rearrange("p (c n) -> p c n", c=KD), aw[:, :, 0:ER],
               aw_hi_done, 1, aw_lo_done)
            lo(aw[:, :, HR + ER:2 * HR], wr_raw[:, :, :], aw[:, :, ER:HR], aw_hi_done, 2, aw_lo_done)
            with pool.Fori(1, GROUPS) as g:
                for j in range(GROUP):
                    lo_w(j, j, GROUP * g + j + 1)

            with pool.Fori(0, TILES // 2) as pair:
                for par in range(2):
                    t = 2 * pair + par
                    for i in range(4):
                        lo(fx_lo[:, par, 2 * i:2 * i + 2, :].rearrange("p c n -> p (c n)"), raw[:, X_SLOT[i], :],
                           fx_hi[:, par, 2 * i:2 * i + 2, :].rearrange("p c n -> p (c n)"),
                           x_hi_done, 4 * t + i + 1, x_lo_done)
                    pool.wait_ge(x_lo_done, 4 * t + 4)
                    for ob in range(KD):
                        pool.wait_ge(stage_free[ob % STAGES], 16 * (KD // STAGES) * t + 16 * (ob // STAGES + 1))
                        nc.gpsimd.tensor_tensor(stage[:, ob % STAGES, :], fx_hi[:, par, ob, :].bitcast(f32),
                                                fx_lo[:, par, ob, :].bitcast(f32), ALU.add).then_inc(x_staged, 1)

        @block.vector
        def _(dve):
            mult, add, eq = ALU.mult, ALU.add, ALU.is_equal

            def lo_af(h):
                dve.wait_ge(af_hi_done, h + 1)
                nc.vector.tensor_tensor(af_lo[:, halves[h]], stage[:, AF_STAGE[h], :],
                                        af_hi[:, halves[h]].bitcast(f32), ALU.subtract).then_inc(af_lo_done, 1)

            def lo_bf(h):
                dve.wait_ge(bf_hi_done, h + 1)
                nc.vector.scalar_tensor_tensor(out=bf_lo[:, halves[h]], in0=stage[:, BF_STAGE[h], :],
                                               scalar=coef[:, 0:1], in1=bf_hi[:, halves[h]].bitcast(f32),
                                               op0=mult, op1=ALU.subtract).then_inc(bf_lo_done, 1)

            def add_ft(h, *chunks):
                for c in chunks:
                    piece = f"F{h}{c // 2}"
                    half = raw[:, slot_of[piece], halves[c % 2]]
                    dve.wait_ge(raw_loaded[slot_of[piece]], loaded[piece])
                    dve.wait_ge(ft_product, KD * h + c + 1)
                    nc.vector.scalar_tensor_tensor(out=half, in0=ps[:, FT_BANK[KD * h + c], :], scalar=SCALING,
                                                   in1=half, op0=mult, op1=add).then_inc(ft_added, 1)

            def lo_ft0(c):
                dve.wait_ge(ft_hi_done, c + 1)
                nc.vector.tensor_tensor(fx_lo[:, 0, c, :], raw[:, slot_of[f"F0{c // 2}"], halves[c % 2]],
                                        fx_hi[:, 0, c, :].bitcast(f32), ALU.subtract).then_inc(ft0_odd_lo, 1)

            def lo_w_front(j):
                dve.wait_ge(w_hi_done, j + 1)
                nc.vector.tensor_tensor(w_lo[:, j, 0:KD // 2, :].rearrange("p c n -> p (c n)"),
                                        raw[:, slot_of[f"W{j}"], 0:KD // 2 * P],
                                        w_hi[:, j, 0:KD // 2, :].rearrange("p c n -> p (c n)").bitcast(f32),
                                        ALU.subtract).then_inc(w_front_lo, 1)

            def lo_m(n, d, h, b):
                cols = m_hi[:, bass.ds(d, 1), h * HALF:(h + 1) * HALF].rearrange("p a n -> p (a n)")
                dst = m_lo[:, bass.ds(d, 1), h * HALF:(h + 1) * HALF].rearrange("p a n -> p (a n)")
                dve.wait_ge(m_hi_done, n + 1)
                nc.vector.tensor_tensor(dst, ps[:, b, :], cols.bitcast(f32), ALU.subtract).then_inc(bank_read, 1)

            lo_af(0)
            lo_bf(0)
            add_ft(0, 0, 1)
            lo_af(1)
            lo_ft0(1)
            lo_bf(1)
            add_ft(0, 2, 3)
            lo_w_front(0)
            add_ft(0, 4)
            lo_ft0(3)
            add_ft(0, 5, 6)
            lo_ft0(5)
            add_ft(0, 7)
            lo_ft0(7)
            lo_w_front(1)
            lo_m(0, 0, 0, M_BANK0[0])
            add_ft(1, 0, 1, 2, 3)
            lo_m(1, 1, 0, M_BANK0[1])
            add_ft(1, 4, 5, 6, 7)
            lo_m(2, 2, 0, M_BANK0[2])
            for e in range(E):
                ins = nc.vector.memset(rank[:, :, e:e + 1], float(E - e))
            ins.then_inc(rank_ready, 1)
            dve.wait_ge(ids_loaded, 16 * P // SEQ)
            nc.vector.tensor_scalar(ids_rank[:, :], ids_raw[:, :], -1.0, float(E), mult, add).then_inc(ids_ready, 1)
            dve.wait_ge(rank_ready, 1)
            dve.wait_ge(ids_ready, 1)
            nc.vector.tensor_tensor(lang[:, :, :], rank[:, :, :],
                                    ids_rank[:, :].unsqueeze(2).to_broadcast([P, ROWS // P, E]), eq)\
              .then_inc(lang_hit, 1)
            dve.wait_ge(lang_hit, 1)
            nc.vector.tensor_scalar(lang[:, :, :], lang[:, :, :], LANG_BIAS, None, mult).then_inc(lang_ready, 1)
            with dve.Fori(1, GROUPS) as g:
                for j in range(GROUP):
                    lo_m(2 * GROUP * g - GROUP + j, GROUP * (g - 1) + j, 1, GROUP + j)
                for j in range(GROUP):
                    lo_m(2 * GROUP * g + j, GROUP * g + j, 0, j)
            for j in range(GROUP):
                lo_m(M_BLOCKS - GROUP + j, KM - GROUP + j, 1, GROUP + j)
            dve.wait_ge(lang_ready, 1)
            dve.wait_ge(bias_loaded, 16)

            def spread(v):
                return v.unsqueeze(2).to_broadcast([P, SUBS, E])

            def choose(t, i, src):
                nc.vector.tensor_reduce(top[:, i, :], src[:, :, :], AX.X, ALU.max).then_inc(top_ready[i], 1)
                dve.wait_ge(top_ready[i], t + 1)
                nc.vector.tensor_tensor(hit[:, i, :, :], src[:, :, :], spread(top[:, i, :]), eq)\
                  .then_inc(hit_ready[i], 1)
                dve.wait_ge(hit_ready[i], t + 1)
                nc.vector.tensor_tensor(score[:, i, :, :], hit[:, i, :, :], rank[:, 0:SUBS, :], mult)\
                  .then_inc(score_ready[i], 1)
                dve.wait_ge(score_ready[i], t + 1)
                nc.vector.tensor_reduce(best[:, i, :], score[:, i, :, :], AX.X, ALU.max).then_inc(best_ready[i], 1)
                dve.wait_ge(best_ready[i], t + 1)
                nc.vector.tensor_tensor((first, second)[i][:, :, :], score[:, i, :, :], spread(best[:, i, :]), eq)\
                  .then_inc(chosen[i], 1)
                dve.wait_ge(chosen[i], t + 1)

            def window(t):
                for s in range(SUBS):
                    dve.wait_ge(h_part_read, SUBS * t + s + 1)
                    nc.vector.tensor_tensor(hl[:, s, :], ps[:, C_BANK[s], 0:HR], h_part[:, s, :], add)\
                      .then_inc(hl_ready, 1)
                dve.wait_ge(hl_ready, SUBS * t + SUBS)
                nc.vector.tensor_tensor(logits[:, :, :], hl[:, :, ER:HR], lang[:, bass.ds(SUBS * t, SUBS), :], add)\
                  .then_inc(logits_ready, 1)
                dve.wait_ge(logits_ready, t + 1)
                choose(t, 0, logits)
                nc.vector.scalar_tensor_tensor(out=rest[:, :, :], in0=first[:, :, :], scalar=BELOW,
                                               in1=logits[:, :, :], op0=mult, op1=add).then_inc(rest_ready, 1)
                dve.wait_ge(rest_ready, t + 1)
                choose(t, 1, rest)
                nc.vector.tensor_tensor(gap[:, :], top[:, 1, :], top[:, 0, :], ALU.subtract).then_inc(gap_ready, 1)
                dve.wait_ge(expo_ready, t + 1)
                nc.vector.tensor_scalar(denom[:, :], expo[:, :], 1.0, None, add).then_inc(denom_ready, 1)
                dve.wait_ge(denom_ready, t + 1)
                nc.vector.reciprocal(inv[:, :], denom[:, :]).then_inc(inv_ready, 1)
                dve.wait_ge(inv_ready, t + 1)
                nc.vector.tensor_scalar(weight[:, 0, :], inv[:, :], SCALING, None, mult).then_inc(weight_ready[0], 1)
                dve.wait_ge(weight_ready[0], t + 1)
                nc.vector.tensor_tensor(weight[:, 1, :], expo[:, :], weight[:, 0, :], mult)\
                  .then_inc(weight_ready[1], 1)
                dve.wait_ge(weight_ready[1], t + 1)
                for i in range(2):
                    ins = nc.vector.tensor_tensor(part[:, i, :, :], (first, second)[i][:, :, :],
                                                  spread(weight[:, i, :]), mult)
                ins.then_inc(part_ready, 1)
                dve.wait_ge(part_ready, t + 1)
                nc.vector.tensor_tensor(gates[:, :, :], part[:, 0, :, :], part[:, 1, :, :], add)\
                  .then_inc(gates_ready, 1)
                dve.wait_ge(gates_ready, t + 1)
                for s in range(SUBS):
                    ins = nc.vector.tensor_tensor(
                        gh[:, s, :].rearrange("p (e r) -> p e r", r=R),
                        hl[:, s, 0:ER].rearrange("p (e r) -> p e r", r=R),
                        gates[:, s, :].unsqueeze(2).to_broadcast([P, E, R]), mult)
                ins.then_inc(gh_ready, 1)
                dve.wait_ge(g_hi_done, t + 1)
                nc.vector.tensor_tensor(g_lo[:, :], ps[:, T_BANK, :], g_hi[:, :].bitcast(f32), ALU.subtract)\
                  .then_inc(g_lo_done, 1)
                for ob in range(KD):
                    dve.wait_ge(out_product, KD * t + ob + 1)
                    dve.wait_ge(x_staged, KD * t + ob + 1)
                    st = stage[:, ob % STAGES, :]
                    nc.vector.scalar_tensor_tensor(out=st, in0=ps[:, ob % 4, :], scalar=bias_col[:, ob:ob + 1],
                                                   in1=st, op0=add, op1=add).then_inc(bank_read, 1)

            with dve.Fori(0, TILES) as t:
                window(t)

        @block.tensor
        def _(pe):
            def ft(h, *chunks):
                for c in chunks:
                    n = KD * h + c
                    before = [m for m in range(n) if FT_BANK[m] == FT_BANK[n]]
                    if before:
                        pe.wait_ge(ft_added, before[-1] + 1)
                    cols, dst = slice(c * P, (c + 1) * P), ps[:, FT_BANK[n], :]
                    pe.wait_ge(bf_hi_done, h + 1)
                    pe.wait_ge(af_hi_done, c // 4 + 1)
                    nc.tensor.matmul(dst, af_hi[:, cols], bf_hi[:, halves[h]], start=True, stop=False)
                    pe.wait_ge(af_lo_done, c // 4 + 1)
                    nc.tensor.matmul(dst, af_lo[:, cols], bf_hi[:, halves[h]], start=False, stop=False)
                    pe.wait_ge(bf_lo_done, h + 1)
                    nc.tensor.matmul(dst, af_hi[:, cols], bf_lo[:, halves[h]], start=False, stop=True)\
                      .then_inc(ft_product, 1)

            def m_block(j, h, b, arriving=False, two_makers=False):
                for c in range(KD):
                    if arriving and h == 0:
                        if c in (2, 4):
                            ft(1, c // 2 + 1)
                        pe.wait_ge(ft_hi_done, c + 1)
                    if h == 0 and two_makers and c % (KD // 2) == 0:
                        pe.wait_ge(w_lo_done if c else w_front_lo, j + 1)
                    if arriving and h == 1:
                        pe.wait_ge(ft1_lo, c + 1)
                    nc.tensor.matmul(ps[:, b, :], w_lo[:, j, c, :], fx_hi[:, h, c, :], start=(c == 0), stop=False)
                    if arriving and h == 0:
                        pe.wait_ge(ft0_odd_lo if c % 2 else ft0_even_lo, c // 2 + 1)
                    nc.tensor.matmul(ps[:, b, :], w_hi[:, j, c, :], fx_lo[:, h, c, :], start=False, stop=False)
                for c in range(KD):
                    ins = nc.tensor.matmul(ps[:, b, :], w_hi[:, j, c, :], fx_hi[:, h, c, :],
                                           start=False, stop=(c == KD - 1))
                ins.then_inc(m_product, 1)

            pe.wait_ge(ident_ready, 1)
            for _ in range(WARM_UP):
                nc.tensor.matmul(ps[:, 7, 0:P], ident[:, :], ident[:, :], start=True, stop=True)
            ft(0, *range(KD))
            ft(1, 0, 1)
            m_block(0, 0, M_BANK0[0], arriving=True, two_makers=True)
            pe.wait_ge(ft_added, KD)
            m_block(1, 0, M_BANK0[1], two_makers=True)
            ft(1, *range(4, KD))
            pe.wait_ge(ft_added, KD + 4)
            pe.wait_ge(w_lo_done, 3)
            m_block(2, 0, M_BANK0[2])
            pe.wait_ge(ft_added, NH * KD)
            for j in range(GROUP):
                m_block(j, 1, GROUP + j, arriving=(j == 0))
            with pe.Fori(1, GROUPS) as g:
                for h in range(NH):
                    for j in range(GROUP):
                        if h == 0:
                            pe.wait_ge(w_lo_done, GROUP * g + j + 1)
                        pe.wait_ge(bank_read, 2 * GROUP * g + GROUP * h + j - 2)
                        m_block(j, h, GROUP * h + j)

            def h_and_logits(t, par, n):
                s, c, low = n // (2 * KD), n // 2 % KD, n % 2
                rows, dst = slice(s * P, (s + 1) * P), ps[:, C_BANK[s], 0:2 * HR]
                if s == 2 and n % (2 * KD) == 0:
                    pe.wait_ge(bank_read, M_BLOCKS)
                if not low:
                    nc.tensor.matmul(dst, fx_hi[:, par, c, rows], aw[:, c, :], start=(c == 0), stop=False)
                    return
                ins = nc.tensor.matmul(dst[:, HR:2 * HR], fx_lo[:, par, c, rows], aw[:, c, 0:HR],
                                       start=False, stop=(c == KD - 1))
                if c == KD - 1:
                    ins.then_inc(h_product, 1)

            def features(t, ob, par):
                cols, dst = slice(ob * P, (ob + 1) * P), ps[:, ob % 4, :]
                pe.wait_ge(bank_read, M_BLOCKS - 3 + KD * t + ob)
                products = [(low, high, c) for c in range(KD) for low, high in ((m_lo, fx_hi), (m_hi, fx_lo))]
                products += [(m_hi, fx_hi, c) for c in range(KD)]
                for i, (m, fx, c) in enumerate(products):
                    nc.tensor.matmul(dst, m[:, c, cols], fx[:, par, c, :], start=(i == 0), stop=False)
                    if ob == 0:
                        for n in range(SUBS * 2 * KD * i // len(products), SUBS * 2 * KD * (i + 1) // len(products)):
                            h_and_logits(t, par, n)

            def turn(t):
                pe.wait_ge(gh_ready, t + 1)
                for s in range(SUBS):
                    ins = nc.tensor.transpose(ps[:, T_BANK, s * P:(s + 1) * P], gh[:, s, :], ident[:, :])
                ins.then_inc(g_turned, 1)

            def ranks(ob):
                cols, dst = slice(ob * P, (ob + 1) * P), ps[:, ob % 4, :]
                nc.tensor.matmul(dst, m_lo[:, KD, cols], g_hi[:, :], start=False, stop=False)
                nc.tensor.matmul(dst, m_hi[:, KD, cols], g_lo[:, :], start=False, stop=False)
                nc.tensor.matmul(dst, m_hi[:, KD, cols], g_hi[:, :], start=False, stop=True)\
                  .then_inc(out_product, 1)

            pe.wait_ge(aw_lo_done, 2)
            with pe.Fori(0, TILES // 2) as pair:
                for par in range(2):
                    t = 2 * pair + par
                    pe.wait_ge(x_lo_done, 4 * t + 4)
                    for ob in range(KD):
                        features(t, ob, par)
                        if ob == 2:
                            turn(t)
                        if ob == 3:
                            pe.wait_ge(g_lo_done, t + 1)
                            for n in range(3):
                                ranks(n)
                        if ob >= 3:
                            ranks(ob)


def kernel(x, itok_B_0_7, L0_cond_W, L0_cond_Wr, L0_cond_A, L0_cond_B, L0_ffn_lora_A, L0_ffn_lora_B, L0_ffn_W,
           L0_ffn_bias, L0_ffn_lora_weights):
    import numpy as np
    import concourse.bacc as bacc
    from concourse.bass_utils import run_bass_kernel_spmd

    n = np.asarray
    xt = n(x).reshape(TILES, TILE, KD // 2, 2, P).transpose(0, 2, 4, 3, 1).reshape(-1, P, 1024)
    w = n(L0_cond_W).reshape(KD, P, KD, P).transpose(2, 1, 0, 3).reshape(KD, P, 1024)
    b = n(L0_cond_B).transpose(1, 0, 2).reshape(KD, P, ER).transpose(1, 0, 2).reshape(1, P, 1024)
    arrays = {
        "x": xt,
        "ids": n(itok_B_0_7).reshape(-1, P // SEQ).T,
        "w_blocks": np.concatenate([w, b]),
        "wr": n(L0_cond_Wr).reshape(E, KD, P).transpose(2, 1, 0),
        "a": n(L0_cond_A).reshape(ER, KD, P).transpose(2, 1, 0).reshape(P, 1024),
        "lora_a": n(L0_ffn_lora_A).reshape(ER, D),
        "lora_b": n(L0_ffn_lora_B).transpose(0, 2, 1).reshape(ER, D),
        "ffn_w": n(L0_ffn_W).reshape(NH, HALF, KD // 2, 2, P).transpose(0, 2, 4, 3, 1).reshape(NH, KD // 2, P, 1024),
        "bias": n(L0_ffn_bias).reshape(KD, P).T,
        "lora_weights": n(L0_ffn_lora_weights),
    }
    nc = bacc.Bacc("TRN2", target_bir_lowering=False, num_devices=1)
    args, given = [], {}
    for name, v in arrays.items():
        v = np.ascontiguousarray(v)
        given[f"in_{name}"] = v
        args.append(nc.dram_tensor(f"in_{name}", v.shape, mybir.dt.from_np(v.dtype), kind="ExternalInput").ap())
    args.append(nc.dram_tensor("out_t", (TILES * KD, P, TILE), mybir.dt.float32, kind="ExternalOutput").ap())
    adaln_ffn(nc, *args)
    got = run_bass_kernel_spmd(nc, [given], core_ids=[0]).results[0]["out_t"]
    return got.reshape(TILES, KD, P, TILE).transpose(0, 3, 1, 2).reshape(n(x).shape)
```
